# Optimizing a Trainium2 kernel written in Bass

```python
import numpy as np
import jax
import jax.numpy as jnp

def _softmax(x, axis=-1):
    return jax.nn.softmax(x, axis=axis)

def _gelu(x):
    return jax.nn.gelu(x, approximate=True)

def _silu(x):
    return jax.nn.silu(x)

def _sigmoid(x):
    return jax.nn.sigmoid(x)

def _layernorm(x, axis=-1, eps=1e-05):
    m = jnp.mean(x, axis=axis, keepdims=True)
    v = jnp.var(x, axis=axis, keepdims=True)
    return (x - m) / jnp.sqrt(v + eps)

def _scatter_add(tgt, idx, src, axis=0):
    return tgt.at[idx].add(src)

def _segment_sum(src, seg, n):
    return jax.ops.segment_sum(src, seg, n)
kernel_name = 'mk_adaln_d2_jaxref_r8_9ab8e8'

def setup_inputs(seed: int=0):
    np.random.seed(seed)
    _w = jnp.asarray

    def _L0_attn_setup():
        import jax, jax.numpy as jnp
        import numpy as np
        B, S, D = (2, 256, 512)
        NH, NKV = (32, 8)
        HD = D // NH
        NREP = NH // NKV
        SCALE = HD ** (-0.5)
        key = jax.random.key(seed)
        kx, kq, kk, kv, ko = jax.random.split(key, 5)
        s = 0.02
        return {'x': jax.random.normal(kx, (B, S, D), dtype=jnp.float32), 'wq': jax.random.normal(kq, (D, NH * HD), dtype=jnp.float32) * s, 'wk': jax.random.normal(kk, (D, NKV * HD), dtype=jnp.float32) * s, 'wv': jax.random.normal(kv, (D, NKV * HD), dtype=jnp.float32) * s, 'wo': jax.random.normal(ko, (NH * HD, D), dtype=jnp.float32) * s}
    _L0_attn_in = _L0_attn_setup()

    def _L0_ffn_setup():
        import jax, jax.numpy as jnp
        import numpy as np
        IN_F = 512
        OUT_F = 512
        RANK = 8
        NUM_EXPERTS = 64
        TOP_K = 16
        ROUTER_DIM = 16
        ALPHA = 32
        SCALING = ALPHA / TOP_K
        BOTTLENECK = NUM_EXPERTS * RANK
        key = jax.random.key(seed)
        ks = jax.random.split(key, 5)
        x = jax.random.normal(ks[0], (4, 512, IN_F), dtype=jnp.float32)
        bound_a = float(np.sqrt(6.0 / IN_F))
        A_w = jax.random.uniform(ks[1], (BOTTLENECK, IN_F), jnp.float32, -bound_a, bound_a)
        B_w = jax.random.normal(ks[2], (OUT_F, BOTTLENECK), dtype=jnp.float32) * 0.02
        Wq_w = jax.random.normal(ks[3], (ROUTER_DIM, IN_F), dtype=jnp.float32) * 0.02
        keys = jax.random.normal(ks[4], (NUM_EXPERTS, ROUTER_DIM), dtype=jnp.float32) * 0.01
        return {'x': x, 'A_w': A_w, 'B_w': B_w, 'Wq_w': Wq_w, 'keys': keys}
    _L0_ffn_in = _L0_ffn_setup()
    _L0_c = _w((lambda *s: np.random.randn(*s).astype(np.float32) * 0.05)(2, 512))
    _L0_wmod = _w((lambda *s: np.random.randn(*s).astype(np.float32) * 0.05)(512, 6 * 512) * 512 ** (-0.5))

    def _L1_attn_setup():
        import jax, jax.numpy as jnp
        import numpy as np
        NF4 = jnp.array([-1.0, -0.6961928009986877, -0.5250730514526367, -0.39491748809814453, -0.28444138169288635, -0.18477343022823334, -0.09105003625154495, 0.0, 0.07958029955625534, 0.16093020141124725, 0.24611230194568634, 0.33791524171829224, 0.44070982933044434, 0.5626170039176941, 0.7229568362236023, 1.0], dtype=jnp.float32)
        BLOCK = 64

        def _dequant(codes, scales):
            w = NF4[codes]
            O, I = w.shape
            w = w.reshape(O, I // BLOCK, BLOCK) * scales[:, :, None]
            return w.reshape(O, I)

        def _lin_lora(x, W, A, B):
            base = jnp.einsum('bsh,oh->bso', x, W)
            lora = jnp.einsum('bsr,or->bso', jnp.einsum('bsh,rh->bsr', x, A), B)
            return base + lora
        H, I, R, BT, S = (512, 1792, 16, 2, 256)
        key = jax.random.key(seed)
        ks = jax.random.split(key, 12)
        x = jax.random.normal(ks[0], (BT, S, H), jnp.float32)
        codes_attn = jax.random.randint(ks[1], (4, H, H), 0, 16, jnp.int32)
        scales_attn = jax.random.uniform(ks[2], (4, H, H // BLOCK), jnp.float32) * 0.02
        codes_gu = jax.random.randint(ks[3], (2, I, H), 0, 16, jnp.int32)
        scales_gu = jax.random.uniform(ks[4], (2, I, H // BLOCK), jnp.float32) * 0.02
        codes_down = jax.random.randint(ks[5], (H, I), 0, 16, jnp.int32)
        scales_down = jax.random.uniform(ks[6], (H, I // BLOCK), jnp.float32) * 0.02
        lora_A_h = jax.random.normal(ks[7], (6, R, H), jnp.float32) * 0.02
        lora_A_down = jax.random.normal(ks[8], (R, I), jnp.float32) * 0.02
        lora_B_attn = jax.random.normal(ks[9], (4, H, R), jnp.float32) * 0.02
        lora_B_gu = jax.random.normal(ks[10], (2, I, R), jnp.float32) * 0.02
        lora_B_down = jax.random.normal(ks[11], (H, R), jnp.float32) * 0.02
        return dict(x=x, codes_attn=codes_attn, scales_attn=scales_attn, codes_gu=codes_gu, scales_gu=scales_gu, codes_down=codes_down, scales_down=scales_down, lora_A_h=lora_A_h, lora_A_down=lora_A_down, lora_B_attn=lora_B_attn, lora_B_gu=lora_B_gu, lora_B_down=lora_B_down)
    _L1_attn_in = _L1_attn_setup()

    def _L1_ffn_setup():
        import jax, jax.numpy as jnp
        import numpy as np
        BLOCK = 64
        NF4_CODE = jnp.array([-1.0, -0.6961928009986877, -0.5250730514526367, -0.39491748809814453, -0.28444138169288635, -0.18477343022823334, -0.09105003625154495, 0.0, 0.07958029955625534, 0.16093020141124725, 0.24611230194568634, 0.33791524171829224, 0.44070982933044434, 0.5626170039176941, 0.7229568362236023, 1.0], dtype=jnp.float32)

        def dequant_nf4(q, absmax, shape):
            w = NF4_CODE[q.reshape(-1)]
            w = w.reshape(-1, BLOCK) * absmax[:, None]
            return w.reshape(shape)
        key = jax.random.key(seed)
        ks = jax.random.split(key, 7)
        HD, M = (512, 1792)
        nblk = HD * M // BLOCK
        x = jax.random.normal(ks[0], (2, 256, HD), dtype=jnp.float32)
        gate_q = jax.random.randint(ks[1], (M, HD), 0, 16, dtype=jnp.int32)
        up_q = jax.random.randint(ks[2], (M, HD), 0, 16, dtype=jnp.int32)
        down_q = jax.random.randint(ks[3], (HD, M), 0, 16, dtype=jnp.int32)
        gate_absmax = jax.random.uniform(ks[4], (nblk,), dtype=jnp.float32) * 0.05
        up_absmax = jax.random.uniform(ks[5], (nblk,), dtype=jnp.float32) * 0.05
        down_absmax = jax.random.uniform(ks[6], (nblk,), dtype=jnp.float32) * 0.05
        return {'x': x, 'gate_q': gate_q, 'gate_absmax': gate_absmax, 'up_q': up_q, 'up_absmax': up_absmax, 'down_q': down_q, 'down_absmax': down_absmax}
    _L1_ffn_in = _L1_ffn_setup()
    _L1_c = _w((lambda *s: np.random.randn(*s).astype(np.float32) * 0.05)(2, 512))
    _L1_wmod = _w((lambda *s: np.random.randn(*s).astype(np.float32) * 0.05)(512, 6 * 512) * 512 ** (-0.5))
    _d = {'L0_attn_x': _L0_attn_in['x'], 'L0_attn_wq': _L0_attn_in['wq'], 'L0_attn_wk': _L0_attn_in['wk'], 'L0_attn_wv': _L0_attn_in['wv'], 'L0_attn_wo': _L0_attn_in['wo'], 'L0_ffn_A_w': _L0_ffn_in['A_w'], 'L0_ffn_B_w': _L0_ffn_in['B_w'], 'L0_ffn_Wq_w': _L0_ffn_in['Wq_w'], 'L0_ffn_keys': _L0_ffn_in['keys'], 'L0_c': _L0_c, 'L0_wmod': _L0_wmod, 'L1_attn_codes_attn': _L1_attn_in['codes_attn'], 'L1_attn_scales_attn': _L1_attn_in['scales_attn'], 'L1_attn_codes_gu': _L1_attn_in['codes_gu'], 'L1_attn_scales_gu': _L1_attn_in['scales_gu'], 'L1_attn_codes_down': _L1_attn_in['codes_down'], 'L1_attn_scales_down': _L1_attn_in['scales_down'], 'L1_attn_lora_A_h': _L1_attn_in['lora_A_h'], 'L1_attn_lora_A_down': _L1_attn_in['lora_A_down'], 'L1_attn_lora_B_attn': _L1_attn_in['lora_B_attn'], 'L1_attn_lora_B_gu': _L1_attn_in['lora_B_gu'], 'L1_attn_lora_B_down': _L1_attn_in['lora_B_down'], 'L1_ffn_gate_q': _L1_ffn_in['gate_q'], 'L1_ffn_gate_absmax': _L1_ffn_in['gate_absmax'], 'L1_ffn_up_q': _L1_ffn_in['up_q'], 'L1_ffn_up_absmax': _L1_ffn_in['up_absmax'], 'L1_ffn_down_q': _L1_ffn_in['down_q'], 'L1_ffn_down_absmax': _L1_ffn_in['down_absmax'], 'L1_c': _L1_c, 'L1_wmod': _L1_wmod}
    _x0 = _d['L0_attn_x']
    _d['L0_attn_x'] = jax.random.normal(jax.random.fold_in(jax.random.key(seed), 1), (2, 512, 512), dtype=_x0.dtype)
    del _x0
    return _d

def reference(L0_attn_x, L0_attn_wq, L0_attn_wk, L0_attn_wv, L0_attn_wo, L0_ffn_A_w, L0_ffn_B_w, L0_ffn_Wq_w, L0_ffn_keys, L0_c, L0_wmod, L1_attn_codes_attn, L1_attn_scales_attn, L1_attn_codes_gu, L1_attn_scales_gu, L1_attn_codes_down, L1_attn_scales_down, L1_attn_lora_A_h, L1_attn_lora_A_down, L1_attn_lora_B_attn, L1_attn_lora_B_gu, L1_attn_lora_B_down, L1_ffn_gate_q, L1_ffn_gate_absmax, L1_ffn_up_q, L1_ffn_up_absmax, L1_ffn_down_q, L1_ffn_down_absmax, L1_c, L1_wmod):

    def _L0_attn_ref(x, wq, wk, wv, wo):
        import jax, jax.numpy as jnp
        import numpy as np
        B, S, D = (2, 256, 512)
        NH, NKV = (32, 8)
        HD = D // NH
        NREP = NH // NKV
        SCALE = HD ** (-0.5)
        b, s, _ = x.shape
        q = (x @ wq).reshape(b, s, NH, HD)
        k = (x @ wk).reshape(b, s, NKV, HD)
        v = (x @ wv).reshape(b, s, NKV, HD)
        k = jnp.repeat(k, NREP, axis=2)
        v = jnp.repeat(v, NREP, axis=2)
        scores = jnp.einsum('bihd,bjhd->bhij', q, k) * SCALE
        causal = jnp.tril(jnp.ones((s, s), dtype=bool))
        scores = jnp.where(causal, scores, jnp.finfo(scores.dtype).min)
        attn = jax.nn.softmax(scores, axis=-1)
        out = jnp.einsum('bhij,bjhd->bihd', attn, v)
        out = out.reshape(b, s, NH * HD)
        return out @ wo

    def _L0_ffn_ref(x, A_w, B_w, Wq_w, keys):
        import jax, jax.numpy as jnp
        import numpy as np
        IN_F = 512
        OUT_F = 512
        RANK = 8
        NUM_EXPERTS = 64
        TOP_K = 16
        ROUTER_DIM = 16
        ALPHA = 32
        SCALING = ALPHA / TOP_K
        BOTTLENECK = NUM_EXPERTS * RANK
        q = jnp.einsum('bsd,rd->bsr', x, Wq_w)
        scores = jnp.einsum('bsr,er->bse', q, keys)
        top_vals, top_idx = jax.lax.top_k(scores, TOP_K)
        top_w = jax.nn.softmax(top_vals, axis=-1)
        gate = jnp.sum(jax.nn.one_hot(top_idx, NUM_EXPERTS, dtype=top_w.dtype) * top_w[..., None], axis=-2)
        z = jnp.einsum('bsd,nd->bsn', x, A_w)
        z = z.reshape(*z.shape[:-1], NUM_EXPERTS, RANK)
        z_gated = (z * gate[..., None]).reshape(*z.shape[:-2], BOTTLENECK)
        out = jnp.einsum('bsn,on->bso', z_gated, B_w) * SCALING
        return out

    def _L1_attn_ref(x, codes_attn, scales_attn, codes_gu, scales_gu, codes_down, scales_down, lora_A_h, lora_A_down, lora_B_attn, lora_B_gu, lora_B_down):
        import jax, jax.numpy as jnp
        import numpy as np
        NF4 = jnp.array([-1.0, -0.6961928009986877, -0.5250730514526367, -0.39491748809814453, -0.28444138169288635, -0.18477343022823334, -0.09105003625154495, 0.0, 0.07958029955625534, 0.16093020141124725, 0.24611230194568634, 0.33791524171829224, 0.44070982933044434, 0.5626170039176941, 0.7229568362236023, 1.0], dtype=jnp.float32)
        BLOCK = 64

        def _dequant(codes, scales):
            w = NF4[codes]
            O, I = w.shape
            w = w.reshape(O, I // BLOCK, BLOCK) * scales[:, :, None]
            return w.reshape(O, I)

        def _lin_lora(x, W, A, B):
            base = jnp.einsum('bsh,oh->bso', x, W)
            lora = jnp.einsum('bsr,or->bso', jnp.einsum('bsh,rh->bsr', x, A), B)
            return base + lora
        q = _lin_lora(x, _dequant(codes_attn[0], scales_attn[0]), lora_A_h[0], lora_B_attn[0])
        k = _lin_lora(x, _dequant(codes_attn[1], scales_attn[1]), lora_A_h[1], lora_B_attn[1])
        v = _lin_lora(x, _dequant(codes_attn[2], scales_attn[2]), lora_A_h[2], lora_B_attn[2])
        attn = (q + k + v) / 3.0
        o = _lin_lora(attn, _dequant(codes_attn[3], scales_attn[3]), lora_A_h[3], lora_B_attn[3])
        x1 = x + o
        g = _lin_lora(x1, _dequant(codes_gu[0], scales_gu[0]), lora_A_h[4], lora_B_gu[0])
        u = _lin_lora(x1, _dequant(codes_gu[1], scales_gu[1]), lora_A_h[5], lora_B_gu[1])
        h = jax.nn.silu(g) * u
        d = _lin_lora(h, _dequant(codes_down, scales_down), lora_A_down, lora_B_down)
        return x1 + d

    def _L1_ffn_ref(x, gate_q, gate_absmax, up_q, up_absmax, down_q, down_absmax):
        import jax, jax.numpy as jnp
        import numpy as np
        BLOCK = 64
        NF4_CODE = jnp.array([-1.0, -0.6961928009986877, -0.5250730514526367, -0.39491748809814453, -0.28444138169288635, -0.18477343022823334, -0.09105003625154495, 0.0, 0.07958029955625534, 0.16093020141124725, 0.24611230194568634, 0.33791524171829224, 0.44070982933044434, 0.5626170039176941, 0.7229568362236023, 1.0], dtype=jnp.float32)

        def dequant_nf4(q, absmax, shape):
            w = NF4_CODE[q.reshape(-1)]
            w = w.reshape(-1, BLOCK) * absmax[:, None]
            return w.reshape(shape)
        HD = x.shape[-1]
        M = gate_q.shape[0]
        Wg = dequant_nf4(gate_q, gate_absmax, (M, HD))
        Wu = dequant_nf4(up_q, up_absmax, (M, HD))
        Wd = dequant_nf4(down_q, down_absmax, (HD, M))
        g = jnp.einsum('bsh,mh->bsm', x, Wg)
        u = jnp.einsum('bsh,mh->bsm', x, Wu)
        h = jax.nn.silu(g) * u
        return jnp.einsum('bsm,hm->bsh', h, Wd)
    x = L0_attn_x
    mod = (_silu(L0_c) @ L0_wmod).reshape(L0_c.shape[0], 6, 1, -1)
    sa, ca, ga, sb, cb, gb = (mod[:, 0], mod[:, 1], mod[:, 2], mod[:, 3], mod[:, 4], mod[:, 5])
    ga = (2 * (ga >= 0) - 1) * jnp.maximum(jnp.abs(ga), 0.25)
    gb = (2 * (gb >= 0) - 1) * jnp.maximum(jnp.abs(gb), 0.25)
    h = _layernorm(x, axis=-1) * (1 + ca) + sa
    x = x + ga * _L0_attn_ref(h, L0_attn_wq, L0_attn_wk, L0_attn_wv, L0_attn_wo)
    h = _layernorm(x, axis=-1) * (1 + cb) + sb
    x = x + gb * _L0_ffn_ref(h, L0_ffn_A_w, L0_ffn_B_w, L0_ffn_Wq_w, L0_ffn_keys)
    mod = (_silu(L1_c) @ L1_wmod).reshape(L1_c.shape[0], 6, 1, -1)
    sa, ca, ga, sb, cb, gb = (mod[:, 0], mod[:, 1], mod[:, 2], mod[:, 3], mod[:, 4], mod[:, 5])
    ga = (2 * (ga >= 0) - 1) * jnp.maximum(jnp.abs(ga), 0.25)
    gb = (2 * (gb >= 0) - 1) * jnp.maximum(jnp.abs(gb), 0.25)
    h = _layernorm(x, axis=-1) * (1 + ca) + sa
    x = x + ga * _L1_attn_ref(h, L1_attn_codes_attn, L1_attn_scales_attn, L1_attn_codes_gu, L1_attn_scales_gu, L1_attn_codes_down, L1_attn_scales_down, L1_attn_lora_A_h, L1_attn_lora_A_down, L1_attn_lora_B_attn, L1_attn_lora_B_gu, L1_attn_lora_B_down)
    h = _layernorm(x, axis=-1) * (1 + cb) + sb
    x = x + gb * _L1_ffn_ref(h, L1_ffn_gate_q, L1_ffn_gate_absmax, L1_ffn_up_q, L1_ffn_up_absmax, L1_ffn_down_q, L1_ffn_down_absmax)
    return x

_drawn_inputs = setup_inputs


def setup_inputs(seed=0):
    import zlib

    import numpy as np

    out = dict(_drawn_inputs(seed))
    spreads = {}
    factors = {'L0_attn_wq': 8.0,
     'L0_attn_wk': 8.0,
     'L0_attn_wv': 8.0,
     'L0_attn_wo': 8.0,
     'L0_ffn_A_w': 5.044,
     'L0_ffn_B_w': 4.613,
     'L0_ffn_Wq_w': 5.442,
     'L0_ffn_keys': 5.465,
     'L0_c': 4.094,
     'L0_wmod': 4.134,
     'L1_attn_scales_attn': 8.0,
     'L1_attn_scales_gu': 8.0,
     'L1_attn_scales_down': 8.0,
     'L1_attn_lora_A_h': 8.0,
     'L1_attn_lora_A_down': 8.0,
     'L1_attn_lora_B_attn': 8.0,
     'L1_attn_lora_B_gu': 8.0,
     'L1_attn_lora_B_down': 8.0,
     'L1_ffn_gate_absmax': 8.0,
     'L1_ffn_up_absmax': 8.0,
     'L1_ffn_down_absmax': 8.0}
    for name, (base, spread) in spreads.items():
        noise = np.random.default_rng([zlib.crc32(name.encode()), seed]).standard_normal(out[name].shape)
        drawn = base * np.exp(spread * noise) if base else spread * noise
        out[name] = jnp.asarray(drawn.astype(out[name].dtype))
    for name, factor in factors.items():
        out[name] = (out[name] * factor).astype(out[name].dtype)
    return out
```

```python
from contextlib import ExitStack

import numpy as np

import concourse.bass as bass
from concourse import mybir

F32 = mybir.dt.float32
F32R = mybir.dt.float32r
BF16 = mybir.dt.bfloat16
I32 = mybir.dt.int32
ALU = mybir.AluOpType
ACT = mybir.ActivationFunctionType
AX_X = mybir.AxisListType.X

P = 128
B, S, D = 2, 512, 512
T = B * S
NT = T // P
TB = S // P
KC = D // P
HEADS, GROUPS = 32, 8
HD = D // HEADS
REP = HEADS // GROUPS
KVW = GROUPS * HD
EXPERTS, RANK, TOPK = 64, 8, 16
ROUTER = 16
MLP = 1792
MC = MLP // P
LR = 16
EPS = 1e-5
MASKED = -1e30

RAMP = [
    (0.30380719900131226, -1.0, -0.5250730514526367),
    (0.13015595078468323, -0.2603122889995575, 0.24063166975975037),
    (0.09966824948787689, -0.39867329597473145, 0.193391352891922),
    (0.09105067700147629, -0.5463047027587891, 0.1706303358078003),
    (0.08518218249082565, -0.685289740562439, 0.1665320098400116),
    (0.10279674828052521, -1.0389612913131714, 0.194597527384758),
    (0.16034144163131714, -1.962531566619873, 0.28224700689315796),
    (0.27704399824142456, -3.8786168098449707, None),
]
PLANES = [7, 1, 2, 3, 4, 5, 6]

PW = 1024
LBW = 256
N_QKV, N_O = 6, 2
GU0, DN0 = 8, 22
GU1, DN1 = 29, 43
PIECES = 50
STACKS = 3
RING = 3
AHEAD = 3


def job_list():
    jobs = []

    def mod(layer):
        for j in range(6):
            jobs.append((("modrow", layer, j), 0))
        jobs.append((("modcol", layer), 0))

    def gates(name):
        for b in range(B):
            jobs.append(((name, b), 0))

    def norm(n):
        for b in range(B):
            for c in range(KC):
                jobs.append((("norm", n, b, c), 1))

    mod(0)
    norm(0)
    for b in range(B):
        for h in range(REP):
            jobs.append((("q", b, h), 1))
        jobs.append((("k", b), 1))
        jobs.append((("v", b), 0))
    mod(1)
    gates("ga0")
    for t in range(NT):
        jobs.append((("wo", t), 0))
    norm(1)
    for b in range(B):
        jobs.append((("rq", b), 0))
    for b in range(B):
        jobs.append((("score", b), 0))
    gates("gb0")
    for i in range(NT + 2):
        if i < NT:
            jobs.append((("z", i), 0))
        if 1 <= i <= NT:
            jobs.append((("zt", i - 1), 1))
        if i >= 2:
            jobs.append((("y", i - 2), 0))
    norm(2)
    for b in range(B):
        jobs.append((("tqkv", b), 1))
        for m in range(KC):
            jobs.append((("qkv", b, m), 1))
    for b in range(B):
        jobs.append((("to", b), 1))
        for m in range(KC):
            jobs.append((("o", b, m), 1))
    for n in range(2):
        if n == 0:
            for b in range(B):
                jobs.append((("tgu", b), 1))
        for m in range(MC):
            for b in range(B):
                for mat in range(2):
                    jobs.append((("gu", n, m, b, mat), 0))
        if n == 0:
            for b in range(B):
                jobs.append((("td", b), 1))
        gates(f"g{n}")
        for t in range(NT):
            jobs.append((("down", n, t), 0))
        if n == 0:
            norm(3)
    return jobs


def build(nc, a, out):
    jobs = job_list()
    J = {key: n for n, (key, _) in enumerate(jobs)}
    CAST = {}
    for n, (key, casts) in enumerate(jobs):
        if casts:
            CAST[key] = len(CAST) + 1

    with ExitStack() as ctx:
        def sem(name):
            return ctx.enter_context(nc.semaphore(name))

        base = nc.sbuf_base
        base = (base + 31) // 32 * 32
        at = [base]

        def sb(name, shape, dt, where=None):
            size = int(np.prod(shape[1:])) * (2 if dt == BF16 else 4)
            if where is None:
                where = at[0]
                at[0] = (where + size + 31) // 32 * 32
            return nc.alloc_sbuf_tensor_at(name, shape, dt, offset=where)

        X = sb("X", [P, NT, D], F32)
        MR = sb("MR", [64, 2, D], F32)
        GAB = sb("GAB", [P, B, D], F32)
        MCOL = sb("MCOL", [P, 2, 4, KC, B], F32)
        ident = sb("ident", [P, P], F32)
        negid = sb("negid", [P, P], F32)
        identR = sb("identR", [P, P], F32R)
        onesR = sb("onesR", [P, P], F32R)
        identB = sb("identB", [P, P], BF16)
        maskB = sb("maskB", [P, P], BF16)
        sel = sb("sel", [64, B, P], F32)
        CT = sb("CT", [P, 2, KC, B], F32)
        SCT = sb("SCT", [P, 2, KC, B], F32)
        ST6 = sb("ST6", [P, TB, 6], F32)
        MV = sb("MV", [P, TB, 2], F32)
        RS = sb("RS", [P, TB], F32)
        SD = sb("SD", [P, TB], F32)
        MX = sb("MX", [P, 2, REP], F32)
        MG = sb("MG", [P, 3, REP], F32)
        HH = sb("HH", [P, KC, T], F32R)
        HL = sb("HL", [P, KC, T], F32R)
        dec0 = at[0]
        CODE = sb("CODE", [P, 2, PW], I32)
        SCALE = sb("SCALE", [P, 2, PW], F32)
        PL = sb("PL", [P, 3, PW], F32)
        ACC = sb("ACC", [P, 2, PW], F32)
        wf0 = at[0]
        WF = sb("WF", [P, 2, PW + LBW], F32)
        R0 = at[0]
        K = 1024
        WM = sb("WM", [P, 3, KC, D], F32, dec0)
        WQKVF = sb("WQKVF", [P, KC, D + 2 * KVW], F32, dec0 + 24 * K)
        WQKVH = sb("WQKVH", [P, KC, D + 2 * KVW], F32R, R0 + 48 * K)
        WQKVL = sb("WQKVL", [P, KC, D + 2 * KVW], F32R, R0 + 60 * K)
        MRT = sb("MRT", [64, 6, D], F32, R0 + 80 * K)
        FH = sb("FH", [P, KC, T], F32R, R0)
        FL = sb("FL", [P, KC, T], F32R, R0 + 16 * K)
        KH = sb("KH", [P, T], F32R, R0 + 32 * K)
        KL = sb("KL", [P, T], F32R, R0 + 36 * K)
        V = sb("V", [P, NT, GROUPS, 2, HD], F32, R0 + 40 * K)
        QS = sb("QS", [P, STACKS, REP, S], F32R, R0 + 76 * K)
        KS = sb("KS", [P, STACKS, S], F32R, dec0 + 40 * K)
        PT = sb("PT", [P, 2, TB, REP, P], F32, R0 + 48 * K)
        DG = sb("DG", [P, 2, REP, P], F32R, R0 + 64 * K)
        OT = sb("OT", [P, 2, S], F32, R0 + 68 * K)
        NUM = sb("NUM", [P, KC, T], F32, dec0 - 32 * K)
        DEN = sb("DEN", [P, KC, T], F32, dec0 - 16 * K)
        WOF = sb("WOF", [P, KC, D], F32, dec0)
        ATF = sb("ATF", [P, KC, D], F32, dec0 + 8 * K)
        BTF = sb("BTF", [P, KC, D], F32, dec0 + 16 * K)
        WOH = sb("WOH", [P, KC, D], F32R, R0 + 48 * K)
        WOL = sb("WOL", [P, KC, D], F32R, R0 + 56 * K)
        ATH = sb("ATH", [P, KC, D], F32R, R0 + 64 * K)
        ATL = sb("ATL", [P, KC, D], F32R, R0 + 72 * K)
        BTH = sb("BTH", [P, KC, D], F32R, R0 + 80 * K)
        BTL = sb("BTL", [P, KC, D], F32R, R0 + 88 * K)
        RQF = sb("RQF", [P, KC, P], F32, wf0)
        RQH = sb("RQH", [P, KC, P], F32R, wf0 + 2 * K)
        RQL = sb("RQL", [P, KC, P], F32R, wf0 + 4 * K)
        KEYS = sb("KEYS", [ROUTER, EXPERTS], F32, wf0 + 6 * K)
        RQ = sb("RQ", [ROUTER, T], F32, R0)
        SCO = sb("SCO", [P, NT, EXPERTS], F32, R0 + 4 * K)
        SC1 = sb("SC1", [P, NT, EXPERTS], F32, R0 + 6 * K)
        SC2 = sb("SC2", [P, NT, EXPERTS], F32, R0 + 8 * K)
        EX = sb("EX", [P, NT, EXPERTS], F32, R0 + 10 * K)
        T8 = sb("T8", [P, NT, 2, 8], F32, R0 + 12 * K)
        NMX = sb("NMX", [P, NT], F32, R0 + 13 * K)
        SUM = sb("SUM", [P, NT], F32, R0 + 13 * K + 64)
        RSUM = sb("RSUM", [P, NT], F32, R0 + 13 * K + 128)
        GATE = sb("GATE", [P, NT, EXPERTS], F32, R0 + 96 * K)
        WS = sb("WS", [P, N_QKV // 3 + N_O, PW], F32, R0 + 32 * K)
        WQH = sb("WQH", [P, KC, D], F32R, R0 + 48 * K)
        WQL = sb("WQL", [P, KC, D], F32R, R0 + 56 * K)
        W2H = sb("W2H", [P, KC, D], F32R, R0 + 64 * K)
        W2L = sb("W2L", [P, KC, D], F32R, R0 + 72 * K)
        TL = sb("TL", [P, T], F32R, R0 + 86 * K)
        LF = sb("LF", [P, KC * P + D], F32, wf0)
        LQ = sb("LQ", [P, 2, KC * P + D], F32R, R0 + 32 * K)
        LOA = sb("LOA", [P, 2, KC * P], F32R, R0 + 80 * K)
        LOB = sb("LOB", [P, 2, D], F32R, R0 + 90 * K)
        LGA = sb("LGA", [P, 2, KC * P], F32R, R0 + 94 * K)
        X1T = sb("X1T", [P, S], F32, R0 + 44 * K)
        HID = sb("HID", [P, MC, T], F32, R0)
        WRH = sb("WRH", [P, RING, PW + LBW], F32R, R0 + 56 * K)
        WRL = sb("WRL", [P, RING, PW + LBW], F32R, R0 + 71 * K)
        SG = sb("SG", [P, 2, S], F32, R0 + 90 * K)
        TDH = sb("TDH", [P, T], F32R, R0 + 86 * K)
        TDL = sb("TDL", [P, T], F32R, R0 + 90 * K)
        LDBF = sb("LDBF", [P, D], F32, R0 + 96 * K)
        LDA = sb("LDA", [P, MC, 2 * LR], F32, R0 + 98 * K)
        LDBH = sb("LDBH", [P, D], F32R, R0 + 94 * K)
        LDBL = sb("LDBL", [P, D], F32R, R0 + 96 * K)
        assert R0 + 100 * K <= nc.sbuf_usable_end, (R0, nc.sbuf_usable_end)
        XN = [sb(f"XN{n}", [P, 3, D], F32, R0 + off * K) for n, off in enumerate((72, 42, 48, 0))]

        PS = ctx.enter_context(nc.psum_tensor("PS", [P, 8, 512], F32))

        def bank(key):
            return J[key] % 8

        s_const = sem("consts_loaded")
        s_c = sem("c_loaded")
        s_x = sem("x_loaded")
        s_wm = [sem(f"wmod_loaded_{i}") for i in range(3)]
        s_wqkv = sem("wqkv_loaded")
        s_l0w = sem("layer0_weights_loaded")
        s_silu = sem("silu_c_ready")
        s_mm = sem("jobs_multiplied")
        s_free = sem("banks_freed")
        s_cast = sem("jobs_rounded")
        s_wqkvh = sem("wqkv_rounded")
        s_wqkvl = sem("wqkv_split")
        s_mr = sem("modulation_rows_ready")
        s_var = sem("variances_ready")
        s_sd = sem("deviations_ready")
        s_xn = sem("tiles_normalised")
        s_xnu = sem("tiles_transposed")
        s_ones = sem("attention_constants_ready")
        s_qks = [sem(f"qk_stack_loaded_{i}") for i in range(STACKS)]
        s_s = sem("scores_ready")
        s_mx = sem("row_maxima_ready")
        s_dg = sem("maxima_diagonal_ready")
        s_st = sem("transposed_scores_ready")
        s_exp = sem("exponentials_ready")
        s_pv = sem("values_weighted")
        s_ot = sem("head_outputs_copied")
        s_num = [sem(f"head_outputs_moved_{i}") for i in range(2)]
        s_div = sem("heads_divided")
        s_oh = sem("heads_rounded")
        s_oL = sem("heads_split")
        s_w0h = sem("layer0_weights_rounded")
        s_w0l = sem("layer0_weights_split")
        s_nmx = sem("router_maxima_ready")
        s_ex = sem("router_exponentials_ready")
        s_code = [sem(f"codes_loaded_{i}") for i in range(2)]
        s_scale = [sem(f"scales_loaded_{i}") for i in range(2)]
        s_plane = sem("ramps_ready")
        s_used = sem("ramps_added")
        s_r0 = sem("first_ramps_ready")
        s_wf = sem("pieces_scaled")
        s_wh = sem("pieces_rounded")
        s_wl = sem("pieces_split")
        s_lora = [sem(f"lora_loaded_{i}") for i in range(3)]
        s_ldw = sem("lora_down_loaded")
        s_ph = sem("projection_weights_rounded")
        s_pl = sem("projection_weights_split")
        s_sg = sem("silu_ready")
        s_hsh = sem("hidden_rounded")
        s_hsl = sem("hidden_split")
        s_hsu = sem("hidden_used")
        s_out_ready = sem("outputs_ready")
        s_out = sem("outputs_stored")
        s_ldh = sem("lora_down_rounded")
        s_x1 = sem("block_sums_ready")
        s_x1u = sem("block_sums_added")
        s_ldl = sem("lora_down_split")
        ch_dve = sem("vector_chain")
        ch_pool = sem("gpsimd_chain")
        ch_act = sem("scalar_chain")

        class Chain:

            def __init__(self, eng, s):
                self.eng, self.s, self.n = eng, s, 0

            def __call__(self, ins):
                self.n += 1
                ins.then_inc(self.s, 1)
                self.eng.wait_ge(self.s, self.n)

        block = ctx.enter_context(nc.Block())
        GU_START = {0: GU0, 1: GU1}
        DN_START = {0: DN0, 1: DN1}
        HS_N = {0: 0, 1: MC}

        def slot(p):
            return (p - GU0) % RING

        def ring_no(p):
            return p - GU0 + 1

        def STC(n):
            return n * (TB * (TB + 1) // 2)

        def load_piece(sp, p):
            if p == 0:
                sp.wait_ge(s_w0l, 4)
            if p >= 2:
                sp.wait_ge(s_plane, 7 * (p - 1))
                sp.wait_ge(s_r0, p - 1)
            sp.dma_start(CODE[:, p % 2], a["CODES"][p]).then_inc(s_code[p % 2], 16)
            if p >= 2:
                sp.wait_ge(s_wf, p - 1)
            for half in range(2):
                sp.dma_start(SCALE[64 * half:64 * half + 64, p % 2],
                             a["SCALES"][p, half:half + 1, :].to_broadcast([64, PW])).then_inc(s_scale[p % 2], 16)
            if GU0 <= p < DN0:
                if p < GU0 + 2:
                    sp.wait_ge(s_pl, 5)
                else:
                    sp.wait_ge(s_wl, ring_no(p) - 2)
                sp.dma_start(WF[:, p % 2, PW:], a["LBGU"][p - GU0]).then_inc(s_scale[p % 2], 16)

        def scale_loads(p):
            n = sum(2 + (GU0 <= q < DN0) for q in range(p % 2, p + 1, 2))
            return 16 * n

        def load_stack(sp, n):
            b, g = divmod(n, GROUPS)
            if n == 0:
                sp.wait_ge(s_ones, 1)
            if g == 0:
                sp.wait_ge(s_free, J["k", b] + 1)
            if n >= STACKS:
                sp.wait_ge(s_st, STC(n - STACKS + 1))
            rows = slice(HD * g, HD * g + HD)
            cols = slice(b * S, b * S + S)
            for r, src in enumerate((FH, FH, FL, FL)):
                sp.dma_start(QS[HD * r:HD * r + HD, n % STACKS].bitcast(F32), src[rows, :, cols].bitcast(F32)
                             ).then_inc(s_qks[n % STACKS], 16)
            for r, src in enumerate((KH, KL, KH, KL)):
                sp.dma_start(KS[HD * r:HD * r + HD, n % STACKS].bitcast(F32), src[rows, cols].bitcast(F32)
                             ).then_inc(s_qks[n % STACKS], 16)

        def move_out(sp, n):
            b, g = divmod(n, GROUPS)
            sp.wait_ge(s_ot, n + 1)
            rows = slice(HD * g, HD * g + HD)
            cols = slice(b * S, b * S + S)
            for h in range(REP):
                sp.dma_start(NUM[rows, h, cols], OT[32 * h:32 * h + HD, n % 2]).then_inc(s_num[n % 2], 16)
                sp.dma_start(DEN[rows, h, cols], OT[32 * h + HD:32 * h + 32, n % 2]).then_inc(s_num[n % 2], 16)

        def copy_heads(act, n):
            act.wait_ge(s_pv, TB * (n + 1))
            if n >= 2:
                act.wait_ge(s_num[n % 2], 128 * (n // 2))
            nc.scalar.activation(OT[:, n % 2], PS[:, 7], ACT.Copy).then_inc(s_ot, 1)


        def weights_used(eng, p):
            for n in range(2):
                if GU_START[n] <= p < DN_START[n]:
                    eng.wait_ge(s_mm, J["gu", n, p - GU_START[n], B - 1, 1] + 1)
                elif DN_START[n] <= p < DN_START[n] + MC // 2:
                    hidden_used(eng, n, 2 * (p - DN_START[n]) + 1)

        def hidden_used(eng, n, k):
            if k < MC - 1:
                eng.wait_ge(s_hsu, (MC - 1) * n + k + 1)
            else:
                eng.wait_ge(s_mm, J["down", n, NT - 1] + 1)

        def tile_transposed(eng, u):
            g, ti = divmod(u, TB)
            if ti < TB - 1:
                eng.wait_ge(s_xnu, (TB - 1) * g + ti + 1)
            else:
                eng.wait_ge(s_mm, J["norm", g // B, g % B, KC - 1] + 1)

        @block.sync
        def _(sp):
            sp.dma_start(CT[:], a["CT"]).then_inc(s_c, 16)
            for l in range(2):
                for j in range(6):
                    n = 6 * l + j
                    if n >= 3:
                        key = ("modrow", (n - 3) // 6, (n - 3) % 6)
                        sp.wait_ge(s_mm, J[key] + 1)
                    sp.dma_start(WM[:, n % 3], a[f"WM{l}"].rearrange("(c p) n -> p c n", p=P)[:, :, j * D:(j + 1) * D]
                                 ).then_inc(s_wm[n % 3], 16)
            for n in range(B * GROUPS + STACKS):
                if n >= STACKS:
                    move_out(sp, n - STACKS)
                if n < B * GROUPS:
                    load_stack(sp, n)
            for p in range(PIECES):
                load_piece(sp, p)
            sp.wait_ge(s_out, 16 * NT)

        @block.gpsimd
        def _(pool):
            link = Chain(pool, ch_pool)
            link(nc.gpsimd.memset(V[:, :, :, 1, :], 1.0))
            pool.wait_ge(s_mm, J["modcol", 1] + 1)
            pool.wait_ge(s_mr, 2)
            link(nc.gpsimd.memset(QS[64:P].rearrange("p a h s -> p (a h s)").bitcast(F32), 0.0))
            nc.gpsimd.memset(KS[64:P].rearrange("p a s -> p (a s)").bitcast(F32), 0.0).then_inc(s_ones, 1)
            pool.wait_ge(s_ones, 1)
            for n in range(B * GROUPS * TB):
                pool.wait_ge(s_mx, 2 * n + 2)
                link(nc.gpsimd.tensor_scalar(MG[:, 0], MX[:, n % 2], 0.0, 2.0 ** -10, ALU.max, ALU.mult))
                link(nc.gpsimd.tensor_scalar(MG[:, 1], MX[:, n % 2], 1.0 - 2.0 ** -11, 0.0, ALU.mult, ALU.add))
                if n >= 1:
                    pool.wait_ge(s_dg, n)
                link(nc.gpsimd.tensor_tensor(MG[:, 2], MG[:, 0], MG[:, 1], ALU.add))
                if n >= 2:
                    done = STC((n - 2) // TB) + sum(i + 1 for i in range((n - 2) % TB + 1))
                    pool.wait_ge(s_st, done)
                nc.gpsimd.tensor_tensor(DG[:, n % 2], negid[:].unsqueeze(1).to_broadcast([P, REP, P]),
                                        MG[:, 2, :].unsqueeze(2).to_broadcast([P, REP, P]), ALU.mult
                                        ).then_inc(s_dg, 1)

            def scale_piece(p):
                pool.wait_ge(s_used, 7 * (p + 1))
                pool.wait_ge(s_scale[p % 2], scale_loads(p))
                acc, sc = ACC[:, p % 2], SCALE[:, p % 2]
                if p < N_QKV:
                    half, mat = divmod(p, 3)
                    if p == 0:
                        pool.wait_ge(s_mm, J["wo", NT - 1] + 1)
                    if mat == 0:
                        nc.gpsimd.tensor_tensor(WS[:, half], acc, sc, ALU.mult).then_inc(s_wf, 1)
                    else:
                        link(nc.gpsimd.tensor_tensor(acc, acc, sc, ALU.mult))
                        pool.wait_ge(s_wf, p)
                        nc.gpsimd.tensor_tensor(WS[:, half], WS[:, half], acc, ALU.add).then_inc(s_wf, 1)
                elif p < GU0:
                    if p == N_QKV:
                        pool.wait_ge(s_mm, J["y", NT - 1] + 1)
                    nc.gpsimd.tensor_tensor(WS[:, p - N_QKV + 2], acc, sc, ALU.mult).then_inc(s_wf, 1)
                else:
                    if p < GU0 + 2:
                        pool.wait_ge(s_pl, 5)
                    else:
                        pool.wait_ge(s_wl, ring_no(p) - 2)
                    nc.gpsimd.tensor_tensor(WF[:, p % 2, 0:PW], acc, sc, ALU.mult).then_inc(s_wf, 1)

            def split_piece(p):
                w = PW + (LBW if GU0 <= p < DN0 else 0)
                pool.wait_ge(s_wh, ring_no(p))
                nc.gpsimd.tensor_tensor(WRL[:, slot(p), 0:w], WF[:, p % 2, 0:w], WRH[:, slot(p), 0:w], ALU.subtract
                                        ).then_inc(s_wl, 1)

            for p in range(GU0):
                scale_piece(p)

            def step(p):
                if p < PIECES:
                    scale_piece(p)
                if GU0 <= p - 1 < PIECES:
                    split_piece(p - 1)

            def hidden_split(n, k):
                i = HS_N[n] + k
                pool.wait_ge(s_hsh, i + 1)
                nc.gpsimd.tensor_tensor(HL[:, k % 4], HID[:, k], HH[:, k % 4], ALU.subtract).then_inc(s_hsl, 1)

            for p in range(GU0, GU0 + AHEAD):
                step(p)
            for n in range(2):
                for m in range(MC):
                    step(GU_START[n] + m + AHEAD)
                for k in range(2):
                    hidden_split(n, k)
                for i in range(MC // 2):
                    if 2 * i + 2 < MC:
                        hidden_split(n, 2 * i + 2)
                        hidden_split(n, 2 * i + 3)
                    step(DN_START[n] + i + AHEAD)

        @block.scalar
        def _(act):
            act.dma_start(X[:], a["X"].rearrange("(t p) d -> p t d", p=P)).then_inc(s_x, 16)
            for dst, name in ((ident, "IDENT"), (negid, "NEGID"), (identB, "IDENTB"), (maskB, "MASKB"), (sel, "SEL")):
                act.dma_start(dst[:], a[name]).then_inc(s_const, 16)
            act.dma_start(WQKVF[:, :, 0:D], a["WQ"].rearrange("(c p) n -> p c n", p=P)).then_inc(s_wqkv, 16)
            act.dma_start(WQKVF[:, :, D:D + KVW], a["WK"].rearrange("(c p) n -> p c n", p=P)).then_inc(s_wqkv, 16)
            act.dma_start(WQKVF[:, :, D + KVW:], a["WV"].rearrange("(c p) n -> p c n", p=P)).then_inc(s_wqkv, 16)
            act.wait_ge(s_c, 16)
            nc.scalar.activation(SCT[:], CT[:], ACT.Silu).then_inc(s_silu, 1)
            act.wait_ge(s_const, 80)
            nc.scalar.activation(identR[:], ident[:], ACT.Copy).then_inc(s_silu, 1)
            nc.scalar.activation(onesR[:], ident[:], ACT.Identity, scale=0.0, bias=1.0).then_inc(s_silu, 1)
            act.wait_ge(s_wqkv, 48)
            nc.scalar.activation(WQKVH[:], WQKVF[:], ACT.Copy).then_inc(s_wqkvh, 1)

            def deviations(n, b):
                act.wait_ge(s_var, 2 * n + b + 1)
                nc.scalar.activation(SD[:], MV[:, :, 1], ACT.Sqrt, bias=EPS).then_inc(s_sd, 1)

            def norm_round(n, b):
                layer, v = divmod(n, 2)
                for c in range(KC):
                    if (b, c) == (0, 0):
                        act.wait_ge(s_mr, layer + 1)
                    act.wait_ge(s_mm, J["norm", n, b, c] + 1)
                    nc.scalar.activation(HH[:, c, b * S:(b + 1) * S], PS[:, bank(("norm", n, b, c))], ACT.Identity,
                                         scale=MCOL[:, layer, 2 * v + 1, c, b:b + 1],
                                         bias=MCOL[:, layer, 2 * v, c, b:b + 1]).then_inc(s_cast, 1)

            def norm(n):
                for b in range(B):
                    deviations(n, b)
                    norm_round(n, b)

            norm(0)
            for b in range(B):
                cols = slice(b * S, (b + 1) * S)
                for h in range(REP):
                    act.wait_ge(s_mm, J["q", b, h] + 1)
                    nc.scalar.activation(FH[:, h, cols], PS[:, bank(("q", b, h))], ACT.Copy).then_inc(s_cast, 1)
                act.wait_ge(s_mm, J["k", b] + 1)
                nc.scalar.activation(KH[:, cols], PS[:, bank(("k", b))], ACT.Copy).then_inc(s_cast, 1)
            done = 0
            for n in range(B * GROUPS * TB):
                ic = n % TB
                if n >= 2:
                    act.wait_ge(s_pv, n - 1)
                for jc in range(ic + 1):
                    act.wait_ge(s_st, done + 1)
                    nc.scalar.activation(PT[:, n % 2, jc].rearrange("p h i -> p (h i)"), PS[:, 4 + done % 3],
                                         ACT.Exp, scale=HD ** -0.5).then_inc(s_exp, 1)
                    done += 1
                if ic == 0 and n:
                    copy_heads(act, n // TB - 1)
            copy_heads(act, B * GROUPS - 1)
            act.wait_ge(s_ot, B * GROUPS)
            act.wait_ge(s_wqkvl, 1)
            act.wait_ge(s_mm, J["modcol", 1] + 1)
            for dst, name in ((WOF, "WO"), (ATF, "AT"), (BTF, "BT")):
                act.dma_start(dst[:], a[name].rearrange("(c p) n -> p c n", p=P)).then_inc(s_l0w, 16)
            act.dma_start(RQF[:], a["RQ"]).then_inc(s_l0w, 16)
            act.dma_start(KEYS[:], a["KEYS"]).then_inc(s_l0w, 16)
            act.wait_ge(s_l0w, 80)
            act.wait_ge(s_pv, B * GROUPS * TB)
            act.wait_ge(s_num[0], 64 * B * GROUPS)
            act.wait_ge(s_num[1], 64 * B * GROUPS)
            act.dma_start(LDA[:], a["LDA"]).then_inc(s_ldw, 16)
            nc.scalar.activation(WOH[:], WOF[:], ACT.Copy).then_inc(s_w0h, 1)
            for b in range(B):
                act.wait_ge(s_div, b + 1)
                nc.scalar.activation(FH[:, :, b * S:(b + 1) * S], NUM[:, :, b * S:(b + 1) * S], ACT.Copy
                                     ).then_inc(s_oh, 1)
            nc.scalar.activation(ATH[:], ATF[:], ACT.Copy).then_inc(s_w0h, 1)
            nc.scalar.activation(BTH[:], BTF[:], ACT.Copy).then_inc(s_w0h, 1)
            nc.scalar.activation(RQH[:], RQF[:], ACT.Copy).then_inc(s_w0h, 1)
            norm(1)
            for t in range(NT):
                act.wait_ge(s_nmx, t + 1)
                nc.scalar.activation(EX[:, t], SCO[:, t], ACT.Exp, bias=NMX[:, t:t + 1]).then_inc(s_ex, 1)

            def planes(p):
                for i, r in enumerate(PLANES):
                    n = 7 * p + i
                    if i == 0:
                        act.wait_ge(s_code[p % 2], 16 * (p // 2 + 1))
                    if n >= 3:
                        act.wait_ge(s_used, n - 2)
                    nc.scalar.activation(PL[:, n % 3], CODE[:, p % 2], ACT.Relu, scale=RAMP[r][0], bias=RAMP[r][1]
                                         ).then_inc(s_plane, 1)

            def round_piece(p):
                w = PW + (LBW if GU0 <= p < DN0 else 0)
                act.wait_ge(s_wf, p + 1)
                if GU0 <= p < DN0:
                    act.wait_ge(s_scale[p % 2], scale_loads(p))
                if p < GU0 + RING:
                    if p == GU0:
                        act.wait_ge(s_mm, J["o", B - 1, KC - 1] + 1)
                else:
                    weights_used(act, p - RING)
                nc.scalar.activation(WRH[:, slot(p), 0:w], WF[:, p % 2, 0:w], ACT.Copy).then_inc(s_wh, 1)

            for t in range(NT):
                act.wait_ge(s_mm, J["zt", t] + 1)
                nc.scalar.activation(FH[:, :, t * P:(t + 1) * P],
                                     PS[:, bank(("zt", t))].rearrange("p (c k) -> p c k", c=KC), ACT.Copy
                                     ).then_inc(s_cast, 1)
                if 1 <= t <= N_QKV:
                    planes(t - 1)
            for p in range(N_QKV, GU0):
                planes(p)
            norm(2)
            act.wait_ge(s_mm, J["y", NT - 1] + 1)
            act.wait_ge(s_free, J["norm", 2, B - 1, KC - 1] + 1)
            act.wait_ge(s_wf, N_QKV)
            nc.scalar.activation(WQH[:].rearrange("p c n -> p (c n)"), WS[:, 0:2].rearrange("p a n -> p (a n)"),
                                 ACT.Copy).then_inc(s_ph, 1)
            act.wait_ge(s_wf, GU0)
            nc.scalar.activation(W2H[:].rearrange("p c n -> p (c n)"), WS[:, 2:4].rearrange("p a n -> p (a n)"),
                                 ACT.Copy).then_inc(s_ph, 1)
            act.wait_ge(s_pl, 1)
            act.dma_start(LF[:], a["LQKV"]).then_inc(s_lora[0], 16)
            act.wait_ge(s_lora[0], 16)
            nc.scalar.activation(LQ[:, 0], LF[:], ACT.Copy).then_inc(s_ph, 1)
            act.wait_ge(s_pl, 3)
            act.dma_start(LF[:], a["LO"]).then_inc(s_lora[1], 16)
            act.wait_ge(s_lora[1], 16)
            nc.scalar.activation(LOA[:, 0], LF[:, 0:KC * P], ACT.Copy).then_inc(ch_act, 1)
            nc.scalar.activation(LOB[:, 0], LF[:, KC * P:], ACT.Copy).then_inc(s_ph, 1)
            act.wait_ge(s_pl, 4)
            act.dma_start(LF[:, 0:KC * P], a["LGA"]).then_inc(s_lora[2], 16)
            act.wait_ge(s_lora[2], 16)
            nc.scalar.activation(LGA[:, 0], LF[:, 0:KC * P], ACT.Copy).then_inc(s_ph, 1)

            def round_inner(key):
                act.wait_ge(s_mm, J[key] + 1)
                nc.scalar.activation(TL[:, key[1] * S:(key[1] + 1) * S], PS[:, bank(key)], ACT.Copy).then_inc(s_cast, 1)

            for b in range(B):
                cols = slice(b * S, (b + 1) * S)
                round_inner(("tqkv", b))
                for m in range(KC):
                    act.wait_ge(s_mm, J["qkv", b, m] + 1)
                    nc.scalar.activation(FH[:, m, cols], PS[:, bank(("qkv", b, m))], ACT.Copy, scale=1.0 / 3.0
                                         ).then_inc(s_cast, 1)
            for b in range(B):
                cols = slice(b * S, (b + 1) * S)
                round_inner(("to", b))
                for m in range(KC):
                    act.wait_ge(s_x1, b * KC + m + 1)
                    nc.scalar.activation(HH[:, m, cols], X1T[:], ACT.Copy).then_inc(s_cast, 1)

            def step(p):
                if p < PIECES:
                    planes(p)
                if GU0 <= p - 1 < PIECES:
                    round_piece(p - 1)

            def round_hidden(n, k):
                i = HS_N[n] + k
                if k < 4:
                    act.wait_ge(s_mm, J["gu", n, MC - 1, B - 1, 1] + 1)
                    if n == 0:
                        act.wait_ge(s_x1u, 1)
                else:
                    hidden_used(act, n, k - 4)
                act.wait_ge(s_free, J["gu", n, k, B - 1, 1] + 1)
                nc.scalar.activation(HH[:, k % 4], HID[:, k], ACT.Copy).then_inc(s_hsh, 1)

            for p in range(GU0, GU0 + AHEAD):
                step(p)
            for b in range(B):
                round_inner(("tgu", b))
            act.wait_ge(s_mm, J["tgu", B - 1] + 1)
            act.wait_ge(s_pl, 5)
            act.dma_start(LDBF[:], a["LDB"]).then_inc(s_ldw, 16)
            for n in range(2):
                for m in range(MC):
                    step(GU_START[n] + m + AHEAD)
                    for b in range(B):
                        i = (n * MC + m) * B + b
                        act.wait_ge(s_mm, J["gu", n, m, b, 0] + 1)
                        if i >= 2:
                            bn, mn, nn = (i - 2) % B, (i - 2) // B % MC, (i - 2) // B // MC
                            act.wait_ge(s_free, J["gu", nn, mn, bn, 1] + 1)
                        nc.scalar.activation(SG[:, i % 2], PS[:, bank(("gu", n, m, b, 0))], ACT.Silu).then_inc(s_sg, 1)
                if n == 0:
                    act.wait_ge(s_ldw, 32)
                    nc.scalar.activation(LDBH[:], LDBF[:], ACT.Copy).then_inc(s_ldh, 1)
                    for b in range(B):
                        act.wait_ge(s_mm, J["td", b] + 1)
                        nc.scalar.activation(TDH[:, b * S:(b + 1) * S], PS[:, bank(("td", b))], ACT.Copy
                                             ).then_inc(s_cast, 1)
                for k in range(2):
                    round_hidden(n, k)
                for i in range(MC // 2):
                    if 2 * i + 2 < MC:
                        round_hidden(n, 2 * i + 2)
                        round_hidden(n, 2 * i + 3)
                    step(DN_START[n] + i + AHEAD)
                if n == 0:
                    norm(3)
            for t in range(NT):
                act.wait_ge(s_out_ready, t + 1)
                act.dma_start(out.rearrange("(t p) d -> t p d", p=P)[t], X[:, t]).then_inc(s_out, 16)

        @block.vector
        def _(dve):
            link = Chain(dve, ch_dve)

            def mod(l):
                rows = slice(32 * l, 32 * l + B)
                for j in range(6):
                    dve.wait_ge(s_mm, J["modrow", l, j] + 1)
                    nc.vector.tensor_copy(MRT[rows, j], PS[0:B, bank(("modrow", l, j))]).then_inc(s_free, 1)
                for w, j in enumerate((2, 5)):
                    dve.wait_ge(s_free, J["modrow", l, 5] + 1)
                    link(nc.vector.tensor_scalar(MR[rows, w], MRT[rows, j], 0.0, 2.0, ALU.is_ge, ALU.mult))
                    link(nc.vector.scalar_tensor_tensor(MRT[rows, j], MRT[rows, j], -1.0, MRT[rows, j], ALU.mult, ALU.max))
                    link(nc.vector.tensor_scalar(MRT[rows, j], MRT[rows, j], 0.25, None, ALU.max))
                    link(nc.vector.scalar_tensor_tensor(MR[rows, w], MR[rows, w], -1.0, MRT[rows, j], ALU.add, ALU.mult))
                dve.wait_ge(s_mm, J["modcol", l] + 1)
                nc.vector.tensor_copy(MCOL[:, l].rearrange("p v c b -> p (v c b)"),
                                      PS[:, bank(("modcol", l)), 0:4 * KC * B]).then_inc(s_free, 1)
                dve.wait_ge(s_free, J["modcol", l] + 1)
                link(nc.vector.tensor_scalar(MCOL[:, l, 1], MCOL[:, l, 1], 1.0, None, ALU.add))
                nc.vector.tensor_scalar(MCOL[:, l, 3], MCOL[:, l, 3], 1.0, None, ALU.add).then_inc(s_mr, 1)
                dve.wait_ge(s_mr, l + 1)

            def stats(ti, t):
                link(nc.vector.bn_stats(ST6[:, ti], X[:, t]))
                ins = nc.vector.bn_aggr(MV[:, ti], ST6[:, ti])
                if ti == TB - 1:
                    ins.then_inc(s_var, 1)
                else:
                    link(ins)

            def normalise(n, b):
                dve.wait_ge(s_sd, B * n + b + 1)
                link(nc.vector.reciprocal(RS[:], SD[:]))
                for ti in range(TB):
                    u = (B * n + b) * TB + ti
                    if u % (B * TB) >= 2:
                        tile_transposed(dve, u - 2)
                    nc.vector.tensor_scalar(XN[n][:, u % 2], X[:, b * TB + ti], MV[:, ti, 0:1], RS[:, ti:ti + 1],
                                            ALU.subtract, ALU.mult).then_inc(s_xn, 1)

            def modulate(n, b):
                layer, v = divmod(n, 2)
                for c in range(KC):
                    key = ("norm", n, b, c)
                    cols = slice(b * S, (b + 1) * S)
                    dve.wait_ge(s_cast, CAST[key])
                    dve.wait_ge(s_free, J[key])
                    link(nc.vector.tensor_scalar(XN[n][:, 2], PS[:, bank(key)], MCOL[:, layer, 2 * v + 1, c, b:b + 1],
                                                 MCOL[:, layer, 2 * v, c, b:b + 1], ALU.mult, ALU.add))
                    nc.vector.tensor_tensor(HL[:, c, cols], XN[n][:, 2], HH[:, c, cols], ALU.subtract
                                            ).then_inc(s_free, 1)

            def rest(dst, key, high, scale=None, rows=slice(0, P)):
                dve.wait_ge(s_mm, J[key] + 1)
                dve.wait_ge(s_cast, CAST[key])
                src = PS[rows, bank(key)]
                if scale is None:
                    ins = nc.vector.tensor_tensor(dst, src, high, ALU.subtract)
                else:
                    ins = nc.vector.scalar_tensor_tensor(dst, src, scale, high, ALU.mult, ALU.subtract)
                ins.then_inc(s_free, 1)

            def gates(name):
                for b in range(B):
                    dve.wait_ge(s_mm, J[name, b] + 1)
                    nc.vector.tensor_copy(GAB[:, b], PS[:, bank((name, b))]).then_inc(s_free, 1)
                dve.wait_ge(s_free, J[name, B - 1] + 1)

            def residual(key, t, scratch):
                dve.wait_ge(s_mm, J[key] + 1)
                nc.vector.tensor_tensor(scratch, PS[:, bank(key)], GAB[:, t // TB], ALU.mult).then_inc(s_free, 1)
                dve.wait_ge(s_free, J[key] + 1)
                return nc.vector.tensor_tensor(X[:, t], X[:, t], scratch, ALU.add)

            def decode(p):
                acc = ACC[:, p % 2]
                dve.wait_ge(s_code[p % 2], 16 * (p // 2 + 1))
                if p >= 2:
                    dve.wait_ge(s_wf, p - 1)
                nc.vector.tensor_scalar(acc, CODE[:, p % 2], RAMP[0][0], RAMP[0][1], ALU.mult, ALU.add
                                        ).then_inc(s_r0, 1)
                dve.wait_ge(s_r0, p + 1)
                for i, r in enumerate(PLANES):
                    n = 7 * p + i
                    dve.wait_ge(s_plane, n + 1)
                    if i == 0:
                        ins = nc.vector.scalar_tensor_tensor(acc, acc, RAMP[0][2], PL[:, n % 3], ALU.min, ALU.add)
                    else:
                        ins = nc.vector.scalar_tensor_tensor(acc, PL[:, n % 3], RAMP[r][2], acc, ALU.min, ALU.add)
                    ins.then_inc(s_used, 1)
                    dve.wait_ge(s_used, n + 1)

            mod(0)
            dve.wait_ge(s_x, 16)
            for b in range(B):
                for ti in range(TB):
                    stats(ti, b * TB + ti)
                normalise(0, b)
                modulate(0, b)
                if b == 0:
                    dve.wait_ge(s_wqkvh, 1)
                    nc.vector.tensor_tensor(WQKVL[:], WQKVF[:], WQKVH[:], ALU.subtract).then_inc(s_wqkvl, 1)
            for b in range(B):
                cols = slice(b * S, (b + 1) * S)
                for h in range(REP):
                    rest(FL[:, h, cols], ("q", b, h), FH[:, h, cols])
                rest(KL[:, cols], ("k", b), KH[:, cols])
                dve.wait_ge(s_mm, J["v", b] + 1)
                nc.vector.tensor_copy(V[:, b * TB:(b + 1) * TB, :, 0, :],
                                      PS[:, bank(("v", b))].rearrange("p (t g d) -> p t g d", t=TB, g=GROUPS)
                                      ).then_inc(s_free, 1)
            mod(1)
            for n in range(B * GROUPS * TB):
                for pair in range(2):
                    dve.wait_ge(s_s, 2 * n + pair + 1)
                    if n >= 2:
                        dve.wait_ge(s_dg, n - 1)
                    w = (n % TB + 1) * P
                    nc.vector.reduce_max(MX[:, n % 2, 2 * pair:2 * pair + 2], PS[:, 2 * pair:2 * pair + 2, 0:w], AX_X
                                         ).then_inc(s_mx, 1)
            dve.wait_ge(s_l0w, 80)
            dve.wait_ge(s_w0h, 1)
            nc.vector.tensor_tensor(WOL[:], WOF[:], WOH[:], ALU.subtract).then_inc(s_w0l, 1)
            for b in range(B):
                cols = slice(b * S, (b + 1) * S)
                for i in range(2):
                    dve.wait_ge(s_num[i], 512 * (b + 1))
                link(nc.vector.reciprocal(DEN[:, :, cols], DEN[:, :, cols]))
                nc.vector.tensor_tensor(NUM[:, :, cols], NUM[:, :, cols], DEN[:, :, cols], ALU.mult).then_inc(s_div, 1)
                dve.wait_ge(s_oh, b + 1)
                nc.vector.tensor_tensor(FL[:, :, cols], NUM[:, :, cols], FH[:, :, cols], ALU.subtract).then_inc(s_oL, 1)
            for i, (dst, raw, high) in enumerate(((ATL, ATF, ATH), (BTL, BTF, BTH), (RQL, RQF, RQH))):
                dve.wait_ge(s_w0h, i + 2)
                nc.vector.tensor_tensor(dst[:], raw[:], high[:], ALU.subtract).then_inc(s_w0l, 1)
            gates("ga0")
            for b in range(B):
                for ti in range(TB):
                    t = b * TB + ti
                    link(residual(("wo", t), t, XN[1][:, 2]))
                    stats(ti, t)
                if b:
                    modulate(1, b - 1)
                normalise(1, b)
            modulate(1, B - 1)
            for b in range(B):
                dve.wait_ge(s_mm, J["rq", b] + 1)
                nc.vector.tensor_copy(RQ[:, b * S:(b + 1) * S], PS[0:ROUTER, bank(("rq", b))]).then_inc(s_free, 1)
            for b in range(B):
                dve.wait_ge(s_mm, J["score", b] + 1)
                nc.vector.tensor_copy(SCO[:, b * TB:(b + 1) * TB].rearrange("p t e -> p (t e)"),
                                      PS[:, bank(("score", b)), 0:TB * EXPERTS]).then_inc(s_free, 1)
            dve.wait_ge(s_free, J["score", B - 1] + 1)
            for t in range(NT):
                link(nc.vector.max(T8[:, t, 0], SCO[:, t]))
                nc.vector.tensor_scalar(NMX[:, t:t + 1], T8[:, t, 0, 0:1], -1.0, None, ALU.mult).then_inc(s_nmx, 1)
                link(nc.vector.match_replace(SC1[:, t], T8[:, t, 0], SCO[:, t], -3e38))
                link(nc.vector.max(T8[:, t, 1], SC1[:, t]))
                link(nc.vector.match_replace(SC2[:, t], T8[:, t, 1], SC1[:, t], -3e38))
            link(nc.vector.tensor_tensor(SC1[:], SC2[:], SCO[:], ALU.not_equal))
            dve.wait_ge(s_ex, NT)
            link(nc.vector.tensor_tensor(EX[:], EX[:], SC1[:], ALU.mult))
            link(nc.vector.reduce_sum(SUM[:], EX[:], AX_X))
            link(nc.vector.reciprocal(RSUM[:], SUM[:]))
            link(nc.vector.tensor_scalar(RSUM[:], RSUM[:], 32.0 / TOPK, None, ALU.mult))
            link(nc.vector.tensor_tensor(GATE[:], EX[:], RSUM[:].unsqueeze(2).to_broadcast([P, NT, EXPERTS]), ALU.mult))
            gates("gb0")
            for i in range(NT + 2):
                if i < NT:
                    if i >= 2:
                        dve.wait_ge(s_mm, J["zt", i - 2] + 1)
                    dve.wait_ge(s_mm, J["z", i] + 1)
                    nc.vector.tensor_tensor(XN[1][:, i % 2].rearrange("p (e r) -> p e r", r=RANK),
                                            PS[:, bank(("z", i))].rearrange("p (e r) -> p e r", r=RANK),
                                            GATE[:, i].unsqueeze(2).to_broadcast([P, EXPERTS, RANK]), ALU.mult
                                            ).then_inc(s_free, 1)
                if 1 <= i <= NT:
                    t = i - 1
                    cols = slice(t * P, (t + 1) * P)
                    dve.wait_ge(s_mm, J["zt", t] + 1)
                    dve.wait_ge(s_cast, CAST["zt", t])
                    nc.vector.tensor_tensor(FL[:, :, cols], PS[:, bank(("zt", t))].rearrange("p (c k) -> p c k", c=KC),
                                            FH[:, :, cols], ALU.subtract).then_inc(s_free, 1)
                if i >= 2:
                    t = i - 2
                    link(residual(("y", t), t, XN[2][:, 2]))
                    if t < N_QKV:
                        decode(t)
            decode(N_QKV)
            decode(N_QKV + 1)
            for b in range(B):
                for ti in range(TB):
                    stats(ti, b * TB + ti)
                normalise(2, b)
                modulate(2, b)
            dve.wait_ge(s_ph, 1)
            nc.vector.tensor_tensor(WQL[:].rearrange("p c n -> p (c n)"), WS[:, 0:2].rearrange("p a n -> p (a n)"),
                                    WQH[:].rearrange("p c n -> p (c n)"), ALU.subtract).then_inc(s_pl, 1)
            dve.wait_ge(s_ph, 2)
            nc.vector.tensor_tensor(W2L[:].rearrange("p c n -> p (c n)"), WS[:, 2:4].rearrange("p a n -> p (a n)"),
                                    W2H[:].rearrange("p c n -> p (c n)"), ALU.subtract).then_inc(s_pl, 1)
            dve.wait_ge(s_ph, 3)
            nc.vector.tensor_tensor(LQ[:, 1], LF[:], LQ[:, 0], ALU.subtract).then_inc(s_pl, 1)
            dve.wait_ge(s_ph, 4)
            dve.wait_ge(ch_act, 1)
            link(nc.vector.tensor_tensor(LOA[:, 1], LF[:, 0:KC * P], LOA[:, 0], ALU.subtract))
            nc.vector.tensor_tensor(LOB[:, 1], LF[:, KC * P:], LOB[:, 0], ALU.subtract).then_inc(s_pl, 1)
            dve.wait_ge(s_ph, 5)
            nc.vector.tensor_tensor(LGA[:, 1], LF[:, 0:KC * P], LGA[:, 0], ALU.subtract).then_inc(s_pl, 1)

            def inner(key):
                cols = slice(key[1] * S, (key[1] + 1) * S)
                rest(TL[64:P, cols], key, TL[64:P, cols], rows=slice(64, P))

            for b in range(B):
                inner(("tqkv", b))
                for m in range(KC):
                    cols = slice(b * S, (b + 1) * S)
                    rest(FL[:, m, cols], ("qkv", b, m), FH[:, m, cols], scale=1.0 / 3.0)
            for b in range(B):
                inner(("to", b))
                for m in range(KC):
                    key, cols = ("o", b, m), slice(b * S, (b + 1) * S)
                    dve.wait_ge(s_mm, J[key] + 1)
                    link(nc.vector.tensor_tensor(X1T[:], PS[:, bank(key)], HH[:, m, cols], ALU.add))
                    nc.vector.tensor_tensor(X1T[:], X1T[:], HL[:, m, cols], ALU.add).then_inc(s_x1, 1)
                    dve.wait_ge(s_cast, CAST[key])
                    nc.vector.tensor_tensor(HL[:, m, cols], X1T[:], HH[:, m, cols], ALU.subtract).then_inc(s_free, 1)
                    dve.wait_ge(s_free, J[key] + 1)
            for p in range(GU0, GU0 + AHEAD):
                decode(p)
            for b in range(B):
                inner(("tgu", b))
            for n in range(2):
                for m in range(MC):
                    decode(GU_START[n] + m + AHEAD)
                    for b in range(B):
                        i = (n * MC + m) * B + b
                        dve.wait_ge(s_mm, J["gu", n, m, b, 1] + 1)
                        dve.wait_ge(s_sg, i + 1)
                        nc.vector.tensor_tensor(HID[:, m, b * S:(b + 1) * S], SG[:, i % 2],
                                                PS[:, bank(("gu", n, m, b, 1))], ALU.mult).then_inc(s_free, 2)
                if n == 0:
                    dve.wait_ge(s_ldh, 1)
                    nc.vector.tensor_tensor(LDBL[:], LDBF[:], LDBH[:], ALU.subtract).then_inc(s_ldl, 1)
                    for b in range(B):
                        cols = slice(b * S, (b + 1) * S)
                        rest(TDL[:, cols], ("td", b), TDH[:, cols])
                gates(f"g{n}")
                for i in range(MC // 2):
                    if DN_START[n] + i + AHEAD < PIECES:
                        decode(DN_START[n] + i + AHEAD)
                for b in range(B):
                    for ti in range(TB):
                        t = b * TB + ti
                        ins = residual(("down", n, t), t, XN[3][:, 2])
                        if n == 0:
                            link(ins)
                            stats(ti, t)
                        else:
                            ins.then_inc(s_out_ready, 1)
                            dve.wait_ge(s_out_ready, t + 1)
                    if n == 0:
                        if b:
                            modulate(3, b - 1)
                        normalise(3, b)
                if n == 0:
                    modulate(3, B - 1)

        @block.tensor
        def _(pe):
            def begin(key):
                if J[key] >= 8:
                    pe.wait_ge(s_free, J[key] - 7)
                return PS[:, bank(key)]

            def product(dst, left, right, start=True, stop=True):
                pairs = [(left(k), right(k)) for k in range(KC)]
                for k, ((lh, ll), (rh, rl)) in enumerate(pairs):
                    nc.tensor.matmul(dst, lh, rh, start=start and k == 0, stop=False)
                    nc.tensor.matmul(dst, ll, rh, start=False, stop=False)
                    ins = nc.tensor.matmul(dst, lh, rl, start=False, stop=stop and k == KC - 1)
                return ins

            def h_cols(cols):
                return lambda k: (HH[:, k, cols], HL[:, k, cols])

            def f_cols(cols):
                return lambda k: (FH[:, k, cols], FL[:, k, cols])

            def pair(hi, lo, cols):
                return lambda k: (hi[:, k, cols], lo[:, k, cols])

            def mod(l):
                for j in range(6):
                    n = 6 * l + j
                    if n == 0:
                        pe.wait_ge(s_silu, 1)
                    dst = begin(("modrow", l, j))
                    pe.wait_ge(s_wm[n % 3], 16 * (n // 3 + 1))
                    for k in range(KC):
                        ins = nc.tensor.matmul(dst[0:B], SCT[:, l, k], WM[:, n % 3, k], start=(k == 0), stop=(k == KC - 1))
                    ins.then_inc(s_mm, 1)
                dst = begin(("modcol", l))
                pe.wait_ge(s_free, J["modrow", l, 5] + 1)
                rows = slice(32 * l, 32 * l + B)
                for v, j in enumerate((0, 1, 3, 4)):
                    for c in range(KC):
                        ins = nc.tensor.transpose(dst[:, (v * KC + c) * B:(v * KC + c + 1) * B],
                                                  MRT[rows, j, c * P:(c + 1) * P], ident[rows, rows])
                ins.then_inc(s_mm, 1)

            def norm(n):
                for b in range(B):
                    dst = [begin(("norm", n, b, c)) for c in range(KC)]
                    for ti in range(TB):
                        u = (B * n + b) * TB + ti
                        pe.wait_ge(s_xn, u + 1)
                        for c in range(KC):
                            ins = nc.tensor.transpose(dst[c][:, ti * P:(ti + 1) * P],
                                                      XN[n][:, u % 2, c * P:(c + 1) * P], ident[:])
                            if ti == TB - 1:
                                ins.then_inc(s_mm, 1)
                        if ti < TB - 1:
                            ins.then_inc(s_xnu, 1)

            def gates(name, l, w):
                for b in range(B):
                    dst = begin((name, b))
                    rows = slice(32 * l, 32 * l + B)
                    nc.tensor.matmul(dst, sel[rows, b], MR[rows, w], start=True, stop=True).then_inc(s_mm, 1)

            pe.wait_ge(s_const, 80)
            mod(0)
            norm(0)
            pe.wait_ge(s_wqkvl, 1)
            for b in range(B):
                cols = slice(b * S, (b + 1) * S)
                pe.wait_ge(s_free, J["norm", 0, b, KC - 1] + 1)
                for h in range(REP):
                    product(begin(("q", b, h)), pair(WQKVH, WQKVL, slice(h * P, (h + 1) * P)), h_cols(cols)
                            ).then_inc(s_mm, 1)
                product(begin(("k", b)), pair(WQKVH, WQKVL, slice(D, D + KVW)), h_cols(cols)).then_inc(s_mm, 1)
                dst = begin(("v", b))
                for ti in range(TB):
                    t = b * TB + ti
                    ins = product(dst[:, ti * P:(ti + 1) * P], h_cols(slice(t * P, (t + 1) * P)),
                                  pair(WQKVH, WQKVL, slice(D + KVW, D + 2 * KVW)))
                ins.then_inc(s_mm, 1)
            mod(1)

            units = B * GROUPS * TB
            pe.wait_ge(s_free, J["ga0", 0])
            pe.wait_ge(s_silu, 3)
            blocks = [0, 0]

            def scores(n):
                q, ic = divmod(n, TB)
                if ic == 0:
                    pe.wait_ge(s_qks[q % STACKS], 128 * (q // STACKS + 1))
                for half in range(2):
                    if n >= 1:
                        pe.wait_ge(s_mx, 2 * (n - 1) + half + 1)
                    for h in (2 * half, 2 * half + 1):
                        nc.tensor.matmul(PS[:, h, 0:(ic + 1) * P], QS[:, q % STACKS, h, ic * P:(ic + 1) * P],
                                         KS[:, q % STACKS, 0:(ic + 1) * P], start=True, stop=True)
                        ins = nc.tensor.matmul(PS[:, h, ic * P:(ic + 1) * P], identB[:], maskB[:], start=False, stop=True,
                                               skip_group_check=True)
                    ins.then_inc(s_s, 1)

            def transposed(n):
                q, ic = divmod(n, TB)
                for jc in range(ic + 1):
                    i = blocks[0]
                    if i >= 3:
                        pe.wait_ge(s_exp, i - 2)
                    dst = PS[:, 4 + i % 3]
                    nc.tensor.matmul(dst, KS[:, q % STACKS, jc * P:(jc + 1) * P], QS[:, q % STACKS, :, ic * P:(ic + 1) * P],
                                     start=True, stop=False)
                    if jc == ic:
                        nc.tensor.matmul(dst, maskB[:], identB[:].unsqueeze(1).to_broadcast([P, REP, P]),
                                         start=False, stop=False)
                    if jc == 0:
                        pe.wait_ge(s_dg, n + 1)
                    nc.tensor.matmul(dst, onesR[:], DG[:, n % 2], start=False, stop=True).then_inc(s_st, 1)
                    blocks[0] += 1

            def weighted(n):
                q, ic = divmod(n, TB)
                b, g = divmod(q, GROUPS)
                if ic == 0 and q:
                    pe.wait_ge(s_ot, q)
                for jc in range(ic + 1):
                    blocks[1] += 1
                    pe.wait_ge(s_exp, blocks[1])
                    for h in range(REP):
                        ins = nc.tensor.matmul(PS[32 * h:32 * h + 32, 7, ic * P:(ic + 1) * P],
                                               V[:, b * TB + jc, g].rearrange("p a d -> p (a d)"), PT[:, n % 2, jc, h],
                                               start=(jc == 0), stop=(jc == ic), tile_position=(0, 32 * h))
                ins.then_inc(s_pv, 1)

            for n in range(units + 3):
                if n < units:
                    scores(n)
                if 2 <= n < units + 2:
                    transposed(n - 2)
                if n >= 3:
                    weighted(n - 3)
            pe.wait_ge(s_mx, 2 * units)
            pe.wait_ge(s_ot, B * GROUPS)
            pe.wait_ge(s_exp, blocks[0])

            gates("ga0", 0, 0)
            pe.wait_ge(s_w0l, 1)
            for t in range(NT):
                if t % TB == 0:
                    pe.wait_ge(s_oL, t // TB + 1)
                product(begin(("wo", t)), f_cols(slice(t * P, (t + 1) * P)), pair(WOH, WOL, slice(0, D))
                        ).then_inc(s_mm, 1)
            norm(1)
            pe.wait_ge(s_w0l, 4)
            for b in range(B):
                pe.wait_ge(s_free, J["norm", 1, b, KC - 1] + 1)
                product(begin(("rq", b)), pair(RQH, RQL, slice(0, P)), h_cols(slice(b * S, (b + 1) * S))
                        ).then_inc(s_mm, 1)
            for b in range(B):
                dst = begin(("score", b))
                pe.wait_ge(s_free, J["rq", b] + 1)
                for ti in range(TB):
                    t = b * TB + ti
                    ins = nc.tensor.matmul(dst[:, ti * EXPERTS:(ti + 1) * EXPERTS], RQ[:, t * P:(t + 1) * P], KEYS[:],
                                           start=True, stop=True)
                ins.then_inc(s_mm, 1)
            gates("gb0", 0, 1)
            for i in range(NT + 2):
                if i < NT:
                    product(begin(("z", i)), h_cols(slice(i * P, (i + 1) * P)), pair(ATH, ATL, slice(0, D))
                            ).then_inc(s_mm, 1)
                if 1 <= i <= NT:
                    dst = begin(("zt", i - 1))
                    pe.wait_ge(s_free, J["z", i - 1] + 1)
                    for c in range(KC):
                        ins = nc.tensor.transpose(dst[:, c * P:(c + 1) * P], XN[1][:, (i - 1) % 2, c * P:(c + 1) * P],
                                                  ident[:])
                    ins.then_inc(s_mm, 1)
                if i >= 2:
                    dst = begin(("y", i - 2))
                    pe.wait_ge(s_free, J["zt", i - 2] + 1)
                    product(dst, f_cols(slice((i - 2) * P, (i - 1) * P)), pair(BTH, BTL, slice(0, D))
                            ).then_inc(s_mm, 1)
            norm(2)

            def inner(key, weights):
                cols = slice(key[1] * S, (key[1] + 1) * S)
                product(begin(key), lambda k: tuple(weights[:, i, k * P:(k + 1) * P] for i in range(2)),
                        (f_cols if key[0] == "to" else h_cols)(cols)).then_inc(s_mm, 1)

            def outer(dst, weights, b):
                nc.tensor.matmul(dst, weights[0], TL[:, b * S:(b + 1) * S], start=False, stop=False)
                return nc.tensor.matmul(dst, weights[1], TL[:, b * S:(b + 1) * S], start=False, stop=True)

            for b in range(B):
                pe.wait_ge(s_free, J["norm", 2, b, KC - 1] + 1)
                if b == 0:
                    pe.wait_ge(s_pl, 3)
                inner(("tqkv", b), LQ)
                for m in range(KC):
                    dst = begin(("qkv", b, m))
                    product(dst, pair(WQH, WQL, slice(m * P, (m + 1) * P)), h_cols(slice(b * S, (b + 1) * S)), stop=False)
                    pe.wait_ge(s_free, J["tqkv", b] + 1)
                    outer(dst, [LQ[:, i, KC * P + m * P:KC * P + (m + 1) * P] for i in range(2)], b).then_inc(s_mm, 1)
            pe.wait_ge(s_pl, 5)
            for b in range(B):
                pe.wait_ge(s_free, J["qkv", b, KC - 1] + 1)
                inner(("to", b), LOA)
                for m in range(KC):
                    dst = begin(("o", b, m))
                    product(dst, pair(W2H, W2L, slice(m * P, (m + 1) * P)), f_cols(slice(b * S, (b + 1) * S)), stop=False)
                    pe.wait_ge(s_free, J["to", b] + 1)
                    outer(dst, [LOB[:, i, m * P:(m + 1) * P] for i in range(2)], b).then_inc(s_mm, 1)
            for b in range(B):
                pe.wait_ge(s_free, J["o", b, KC - 1] + 1)
                inner(("tgu", b), LGA)
            for n in range(2):
                for m in range(MC):
                    p = GU_START[n] + m
                    pe.wait_ge(s_wl, ring_no(p))
                    for b in range(B):
                        if n and m == 0:
                            pe.wait_ge(s_free, J["norm", 3, b, KC - 1] + 1)
                        for mat in range(2):
                            dst = begin(("gu", n, m, b, mat))

                            def w(k):
                                off = (mat * KC + k) * P
                                return WRH[:, slot(p), off:off + P], WRL[:, slot(p), off:off + P]

                            ins = product(dst, w, h_cols(slice(b * S, (b + 1) * S)), stop=bool(n))
                            if n == 0:
                                pe.wait_ge(s_free, J["tgu", B - 1] + 1)
                                off = PW + mat * P
                                ins = outer(dst, [r[:, slot(p), off:off + P] for r in (WRH, WRL)], b)
                            ins.then_inc(s_mm, 1)
                if n == 0:
                    pe.wait_ge(s_ldw, 16)
                    pe.wait_ge(s_free, J["gu", n, MC - 1, B - 1, 1] + 1)
                    for b in range(B):
                        dst = begin(("td", b))
                        for k in range(MC):
                            q = 32 * (k % 4)
                            ins = nc.tensor.matmul(dst[q:q + 32], LDA[:, k], HID[:, k, b * S:(b + 1) * S],
                                                   start=(k < 4), stop=(k >= MC - 4), tile_position=(0, q))
                        ins.then_inc(s_mm, 1)
                gates(f"g{n}", 1, n)
                dst = [begin(("down", n, t)) for t in range(NT)]
                if n == 0:
                    for t in range(NT):
                        for part in (HH, HL):
                            for c in range(KC):
                                ins = nc.tensor.matmul(dst[t][:, c * P:(c + 1) * P], part[:, c, t * P:(t + 1) * P],
                                                       identR[:], start=(part is HH and c == 0), stop=False,
                                                       skip_group_check=True)
                    ins.then_inc(s_x1u, 1)
                for k in range(MC):
                    p = DN_START[n] + k // 2
                    pe.wait_ge(s_wl, ring_no(p))
                    pe.wait_ge(s_hsl, HS_N[n] + k + 1)
                    w = slice(k % 2 * D, (k % 2 + 1) * D)
                    for t in range(NT):
                        cols = slice(t * P, (t + 1) * P)
                        hh, hl = HH[:, k % 4, cols], HL[:, k % 4, cols]
                        wh, wl = WRH[:, slot(p), w], WRL[:, slot(p), w]
                        last = k == MC - 1
                        nc.tensor.matmul(dst[t], hh, wh, start=(n == 1 and k == 0), stop=False, skip_group_check=True)
                        nc.tensor.matmul(dst[t], hh, wl, start=False, stop=False, skip_group_check=True)
                        ins = nc.tensor.matmul(dst[t], hl, wh, start=False, stop=last and n == 1, skip_group_check=True)
                        if last and n == 0:
                            if t == 0:
                                pe.wait_ge(s_ldl, 1)
                                pe.wait_ge(s_free, J["td", B - 1] + 1)
                            nc.tensor.matmul(dst[t], TDH[:, cols], LDBH[:], start=False, stop=False,
                                             skip_group_check=True)
                            nc.tensor.matmul(dst[t], TDL[:, cols], LDBH[:], start=False, stop=False,
                                             skip_group_check=True)
                            ins = nc.tensor.matmul(dst[t], TDH[:, cols], LDBL[:], start=False, stop=True,
                                                   skip_group_check=True)
                        if last:
                            ins.then_inc(s_mm, 1)
                    if not last:
                        ins.then_inc(s_hsu, 1)
                if n == 0:
                    norm(3)


def layout(x):
    def f(name):
        return np.asarray(x[name])

    def pad_cols(m, copies, width):
        out = np.zeros((m.shape[0], P), m.dtype)
        for off in copies:
            out[:, off:off + m.shape[1]] = m
        return out.reshape(-1, P, P).transpose(1, 0, 2)

    def pad_rows(m, copies):
        out = np.zeros((P, m.shape[1]), m.dtype)
        for off in copies:
            out[off:off + m.shape[0]] = m
        return out

    halves, quadrants = (0, 64), (0, 32, 64, 96)
    r = {"X": f("L0_attn_x").reshape(T, D)}
    r["WQ"] = f("L0_attn_wq").reshape(D, GROUPS, REP, HD).transpose(0, 2, 1, 3).reshape(D, D)
    r["WK"], r["WV"] = f("L0_attn_wk"), f("L0_attn_wv")
    r["WO"] = f("L0_attn_wo").reshape(GROUPS, REP, HD, D).transpose(1, 0, 2, 3).reshape(D, D)
    r["AT"], r["BT"] = f("L0_ffn_A_w").T, f("L0_ffn_B_w").T
    r["RQ"] = pad_cols(f("L0_ffn_Wq_w").T, (0,), P)
    r["KEYS"] = f("L0_ffn_keys").T
    r["CT"] = np.stack([f(f"L{l}_c").T.reshape(KC, P, B).transpose(1, 0, 2) for l in range(2)], 1)
    r["WM0"], r["WM1"] = f("L0_wmod"), f("L1_wmod")

    def attn(codes):
        return codes.reshape(D, 2, 2, P).transpose(1, 3, 2, 0).reshape(2, P, PW)

    def attn_s(s):
        return s.reshape(D, 2, 2, 2).transpose(1, 3, 2, 0).reshape(2, 2, PW)

    def gu(g, u):
        return np.stack([g, u]).reshape(2, MC, P, KC, P).transpose(1, 4, 0, 3, 2).reshape(MC, P, PW)

    def gu_s(g, u):
        return np.stack([g, u]).reshape(2, MC, P, KC, 2).transpose(1, 4, 0, 3, 2).reshape(MC, 2, PW)

    def down(w):
        return w.reshape(D, MC // 2, 2, P).transpose(1, 3, 2, 0).reshape(MC // 2, P, PW)

    def down_s(s):
        return s.reshape(D, MC // 2, 2, 2).transpose(1, 3, 2, 0).reshape(MC // 2, 2, PW)

    ca, sa = f("L1_attn_codes_attn"), f("L1_attn_scales_attn")
    ac, asc = [attn(ca[i]) for i in range(4)], [attn_s(sa[i]) for i in range(4)]
    cg, sg = f("L1_attn_codes_gu"), f("L1_attn_scales_gu")
    per = D // 64
    r["CODES"] = np.concatenate(
        [np.stack([ac[m][h] for h in range(2) for m in range(3)]), ac[3], gu(cg[0], cg[1]),
         down(f("L1_attn_codes_down")), gu(f("L1_ffn_gate_q"), f("L1_ffn_up_q")), down(f("L1_ffn_down_q"))])
    r["SCALES"] = np.concatenate(
        [np.stack([asc[m][h] for h in range(2) for m in range(3)]), asc[3], gu_s(sg[0], sg[1]),
         down_s(f("L1_attn_scales_down")),
         gu_s(f("L1_ffn_gate_absmax").reshape(MLP, per), f("L1_ffn_up_absmax").reshape(MLP, per)),
         down_s(f("L1_ffn_down_absmax").reshape(D, MLP // 64))])
    A, Bm = f("L1_attn_lora_A_h"), f("L1_attn_lora_B_attn")
    cat = np.concatenate
    r["LQKV"] = cat([pad_cols(cat(list(A[0:3])).T, halves, P).reshape(P, KC * P),
                     pad_rows(cat([Bm[i].T for i in range(3)]), halves)], 1)
    r["LO"] = cat([pad_cols(A[3].T, halves, P).reshape(P, KC * P), pad_rows(Bm[3].T, halves)], 1)
    r["LGA"] = pad_cols(cat([A[4], A[5]]).T, halves, P).reshape(P, KC * P)
    bg = f("L1_attn_lora_B_gu")
    lb = np.zeros((P, 2, MLP), bg.dtype)
    for off in halves:
        for mat in range(2):
            lb[off + LR * mat:off + LR * (mat + 1), mat] = bg[mat].T
    r["LBGU"] = lb.reshape(P, 2, MC, P).transpose(2, 0, 1, 3).reshape(MC, P, LBW)
    ad = f("L1_attn_lora_A_down")
    lda = np.zeros((P, MC, 2 * LR), ad.dtype)
    lda[:, :, 0:LR] = ad.T.reshape(MC, P, LR).transpose(1, 0, 2)
    r["LDA"] = lda
    r["LDB"] = pad_rows(f("L1_attn_lora_B_down").T, quadrants)
    eye = np.eye(P, dtype=np.float32)
    r["IDENT"], r["NEGID"] = eye, -eye
    sel = np.zeros((64, B, P), np.float32)
    for l in range(2):
        for b in range(B):
            sel[32 * l + b, b] = 1.0
    r["SEL"] = sel
    bf16 = mybir.dt.np(BF16)
    r["IDENTB"] = eye.astype(bf16)
    r["MASKB"] = np.where(np.arange(P)[None, :] > np.arange(P)[:, None], MASKED, 0.0).astype(bf16)
    return {k: np.ascontiguousarray(v) for k, v in r.items()}


def kernel(**inputs):
    import concourse.bacc as bacc
    from concourse.bass_utils import run_bass_kernel_spmd

    nc = bacc.Bacc("TRN2", target_bir_lowering=False, num_devices=1)
    arrays = layout(inputs)
    a = {k: nc.dram_tensor(f"in_{k}", v.shape, mybir.dt.from_np(v.dtype), kind="ExternalInput").ap()
         for k, v in arrays.items()}
    out = nc.dram_tensor("out_x", (T, D), F32, kind="ExternalOutput").ap()
    build(nc, a, out)
    r = run_bass_kernel_spmd(nc, [{f"in_{k}": v for k, v in arrays.items()}], core_ids=[0])
    return r.results[0]["out_x"].reshape(B, S, D)
```

```python
from contextlib import ExitStack

import numpy as np

import concourse.bass as bass
from concourse import mybir

F32 = mybir.dt.float32
F32R = mybir.dt.float32r
BF16 = mybir.dt.bfloat16
I32 = mybir.dt.int32
ALU = mybir.AluOpType
ACT = mybir.ActivationFunctionType
AX_X = mybir.AxisListType.X

P = 128
B, S, D = 2, 512, 512
T = B * S
NT = T // P
TB = S // P
KC = D // P
HEADS, GROUPS = 32, 8
HD = D // HEADS
REP = HEADS // GROUPS
KVW = GROUPS * HD
EXPERTS, RANK, TOPK, ALPHA = 64, 8, 16, 32
ROUTER = 16
MLP = 1792
MC = MLP // P
LR = 16
EPS = 1e-5
MASKED = -1e30

COLS = [0, 1, 3, 4]
FIRST = [0, 1]
OTHER_ROWS = [(0, j) for j in range(2, 6)] + [(1, j) for j in range(6)]

RAMP = [
    (0.30380719900131226, -1.0, -0.5250730514526367),
    (0.13015595078468323, -0.2603122889995575, 0.24063166975975037),
    (0.09966824948787689, -0.39867329597473145, 0.193391352891922),
    (0.09105067700147629, -0.5463047027587891, 0.1706303358078003),
    (0.08518218249082565, -0.685289740562439, 0.1665320098400116),
    (0.10279674828052521, -1.0389612913131714, 0.194597527384758),
    (0.16034144163131714, -1.962531566619873, 0.28224700689315796),
    (0.27704399824142456, -3.8786168098449707, None),
]
PLANES = [7, 1, 2, 3, 4, 5, 6]

PW = 1024
LBW = 256
N_QKV, N_O = 6, 2
GU0, DN0 = 8, 22
GU1, DN1 = 29, 43
PIECES = 50
PIECES_AT = {2: (0, 1), 5: (2,), 7: (3,), 10: (4,), 12: (5,)}
STACKS = 3
RING = 3
LAG = 4
HALF = 4
AHEAD = 3


HEADS0_AT = [40, 44, 48, 52]


def ramp_at(n):
    if not 0 <= n < B * GROUPS * TB or n % 4 == 3:
        return None
    return divmod(n // 4 * 3 + n % 4, 8)


PROJECTIONS = [key for b in range(B) for key in [("q", b, h) for h in range(REP)] + [("vt", b), ("k", b), ("v", b)]]


def row_after(i):
    return OTHER_ROWS[i:i + 1]


def column_after(i):
    return [row for row in (row_after(i - 1) if i else []) if row[1] in COLS]


def job_list():
    jobs = []

    def mod(layer, js):
        for j in js:
            jobs.append((("modrow", layer, j), 0))
        for j in js:
            jobs.append((("modcol", layer, j), 0))

    def gates(name):
        for b in range(B):
            jobs.append(((name, b), 0))

    def norm(n):
        for b in range(B):
            for c in range(KC):
                jobs.append((("norm", n, b, c), 1))

    mod(0, FIRST)
    norm(0)
    for i, key in enumerate(PROJECTIONS):
        jobs.append((key, key[0] in "qk"))
        jobs.extend((("modrow",) + row, 0) for row in row_after(i))
        jobs.extend((("modcol",) + row, 0) for row in column_after(i))
    jobs.append((("gsum",), 0))
    gates("ga0")
    for t in range(NT):
        jobs.append((("wo", t), 0))
    norm(1)
    for b in range(B):
        jobs.append((("rq", b), 0))
    for b in range(B):
        jobs.append((("score", b), 0))
    gates("gb0")
    for i in range(NT + LAG + 1):
        if i < NT:
            jobs.append((("z", i), 0))
        if 0 <= i - LAG < NT:
            jobs.append((("zt", i - LAG), 1))
        if i > LAG:
            jobs.append((("y", i - LAG - 1), 0))
    norm(2)
    for b in range(B):
        jobs.append((("tqkv", b), 1))
        for m in range(KC):
            jobs.append((("qkv", b, m), 1))
    for b in range(B):
        jobs.append((("to", b), 1))
        for m in range(KC):
            jobs.append((("o", b, m), 1))
    for n in range(2):
        if n == 0:
            for b in range(B):
                jobs.append((("tgu", b), 1))
        for m in range(MC):
            for b in range(B):
                for mat in range(2):
                    jobs.append((("gu", n, m, b, mat), 0))
        if n == 0:
            for b in range(B):
                jobs.append((("td", b), 1))
        gates(f"g{n}")
        for t in range(NT):
            jobs.append((("down", n, t), 0))
        if n == 0:
            norm(3)
    return jobs


def build(nc, a, out):
    jobs = job_list()
    J = {key: n for n, (key, _) in enumerate(jobs)}
    CAST = {}
    for n, (key, casts) in enumerate(jobs):
        if casts:
            CAST[key] = len(CAST) + 1

    with ExitStack() as ctx:
        def sem(name):
            return ctx.enter_context(nc.semaphore(name))

        base = nc.sbuf_base
        base = (base + 31) // 32 * 32
        at = [base]

        def sb(name, shape, dt, where=None):
            size = int(np.prod(shape[1:])) * (2 if dt == BF16 else 4)
            if where is None:
                where = at[0]
                at[0] = (where + size + 31) // 32 * 32
            return nc.alloc_sbuf_tensor_at(name, shape, dt, offset=where)

        X = sb("X", [P, NT, D], F32)
        MR = sb("MR", [P, D], F32)
        gab0 = at[0]
        GAB = sb("GAB", [P, B, D], F32)
        MCOL = sb("MCOL", [P, 2, 4, KC, B], F32)
        ident = sb("ident", [P, P], F32)
        identR = sb("identR", [P, P], F32R)
        onesR = sb("onesR", [P, P], F32R)
        identB = sb("identB", [P, P], BF16)
        maskB = sb("maskB", [P, P], BF16)
        sel = sb("sel", [P, B, P], F32)
        sumsel = sb("sumsel", [P, 32], F32)
        CT = sb("CT", [P, 2, KC, B], F32)
        ST6 = sb("ST6", [P, NT, 6], F32)
        MV = sb("MV", [P, NT, 2], F32)
        RS = sb("RS", [P, NT], F32)
        SD = sb("SD", [P, NT], F32)
        MX = sb("MX", [P, 2, REP], F32)
        MG = sb("MG", [P, 3, REP], F32)
        HH = sb("HH", [P, KC, T], F32R)
        HL = sb("HL", [P, KC, T], F32R)
        dec0 = at[0]
        CODE = sb("CODE", [P, 2, PW], I32)
        SCALE = sb("SCALE", [P, 2, PW], F32)
        PL = sb("PL", [P, 3, PW], F32)
        ACC = sb("ACC", [P, 2, PW], F32)
        wf0 = at[0]
        WF = sb("WF", [P, 2, PW + LBW], F32)
        R0 = at[0]
        K = 1024
        WM = sb("WM", [P, 3, KC, D], F32, dec0)
        WQKVF = sb("WQKVF", [P, KC, D + 2 * KVW], F32, dec0 + 24 * K)
        WQKVH = sb("WQKVH", [P, KC, D + 2 * KVW], F32R, R0 + 48 * K)
        WQKVL = sb("WQKVL", [P, KC, D + 2 * KVW], F32R, R0 + 60 * K)
        SCT = sb("SCT", [P, 2, KC, 32], F32, wf0)
        MRT = sb("MRT", [P, 2, D], F32, gab0)
        MRG = sb("MRG", [P, 4, D], F32, dec0 + 24 * K)
        GR = sb("GR", [P, D], F32, R0 + 72 * K)
        VT = sb("VT", [P, S], F32, R0 + 74 * K)
        FH = sb("FH", [P, KC, T], F32R, R0)
        FL = sb("FL", [P, KC, T], F32R, R0 + 16 * K)
        KH = sb("KH", [P, T], F32R, R0 + 32 * K)
        KL = sb("KL", [P, T], F32R, R0 + 36 * K)
        V = sb("V", [P, NT, GROUPS, 2, HD], F32, R0 + 40 * K)
        QS = sb("QS", [P, STACKS, REP, S], F32R, R0 + 76 * K)
        KS = sb("KS", [P, STACKS, S], F32R, dec0 + 40 * K)
        PT = sb("PT", [P, 2, TB, REP, P], F32, R0 + 48 * K)
        DG = sb("DG", [P, 2, REP, P], F32R, R0 + 64 * K)
        OT = sb("OT", [P, 2, S], F32, R0 + 68 * K)
        WT = [sb("WT0", [P, PW], F32, R0 + 72 * K), sb("WT1", [P, PW], F32, wf0)]
        NUM = sb("NUM", [P, KC, T], F32, dec0 - 32 * K)
        DEN = sb("DEN", [P, KC, T], F32, dec0 - 16 * K)
        WOF = sb("WOF", [P, KC, D], F32, dec0)
        ATF = sb("ATF", [P, KC, D], F32, dec0 + 8 * K)
        BTF = sb("BTF", [P, KC, D], F32, dec0 + 16 * K)
        WOH = sb("WOH", [P, KC, D], F32R, R0 + 48 * K)
        WOL = sb("WOL", [P, KC, D], F32R, R0 + 56 * K)
        ATH = sb("ATH", [P, KC, D], F32R, R0 + 64 * K)
        ATL = sb("ATL", [P, KC, D], F32R, R0 + 72 * K)
        BTH = sb("BTH", [P, KC, D], F32R, R0 + 80 * K)
        BTL = sb("BTL", [P, KC, D], F32R, R0 + 88 * K)
        RQF = sb("RQF", [P, KC, P], F32, wf0)
        RQH = sb("RQH", [P, KC, P], F32R, wf0 + 2 * K)
        RQL = sb("RQL", [P, KC, P], F32R, wf0 + 4 * K)
        KEYS = sb("KEYS", [ROUTER, EXPERTS], F32, wf0 + 6 * K)
        RQ = sb("RQ", [ROUTER, T], F32, R0)
        SCO = sb("SCO", [P, NT, EXPERTS], F32, R0 + 4 * K)
        SC1 = sb("SC1", [P, NT, EXPERTS], F32, R0 + 6 * K)
        SC2 = sb("SC2", [P, NT, EXPERTS], F32, R0 + 8 * K)
        EX = sb("EX", [P, NT, EXPERTS], F32, R0 + 10 * K)
        T8 = sb("T8", [P, NT, 2, 8], F32, R0 + 12 * K)
        NMX = sb("NMX", [P, NT], F32, R0 + 13 * K)
        SUM = sb("SUM", [P, NT], F32, R0 + 13 * K + 64)
        RSUM = sb("RSUM", [P, NT], F32, R0 + 13 * K + 128)
        GATE = sb("GATE", [P, NT, EXPERTS], F32, R0 + 96 * K)
        WSQ = sb("WSQ", [P, 2, PW], F32, R0 + 32 * K)
        WQH = sb("WQH", [P, KC, D], F32R, R0 + 48 * K)
        WQL = sb("WQL", [P, KC, D], F32R, R0 + 56 * K)
        W2H = sb("W2H", [P, KC, D], F32R, R0 + 64 * K)
        W2L = sb("W2L", [P, KC, D], F32R, R0 + 72 * K)
        TL = sb("TL", [P, T], F32R, R0 + 86 * K)
        LF = sb("LF", [P, KC * P + D], F32, wf0)
        LQ = sb("LQ", [P, 2, KC * P + D], F32R, R0 + 32 * K)
        LOA = sb("LOA", [P, 2, KC * P], F32R, R0 + 80 * K)
        LOB = sb("LOB", [P, 2, D], F32R, R0 + 90 * K)
        LGA = sb("LGA", [P, 2, KC * P], F32R, R0 + 94 * K)
        X1T = sb("X1T", [P, S], F32, R0 + 44 * K)
        HID = sb("HID", [P, MC, T], F32, R0)
        WRH = sb("WRH", [P, RING, PW + LBW], F32R, R0 + 56 * K)
        WRL = sb("WRL", [P, RING, PW + LBW], F32R, R0 + 71 * K)
        SG = sb("SG", [P, 2, S], F32, R0 + 90 * K)
        TDH = sb("TDH", [P, T], F32R, R0 + 86 * K)
        TDL = sb("TDL", [P, T], F32R, R0 + 90 * K)
        LDBF = sb("LDBF", [P, D], F32, R0 + 96 * K)
        LDA = sb("LDA", [P, MC, 2 * LR], F32, R0 + 98 * K)
        LDBH = sb("LDBH", [P, D], F32R, R0 + 94 * K)
        LDBL = sb("LDBL", [P, D], F32R, R0 + 96 * K)
        SCR = sb("SCR", [P, 2, D], F32, R0 + 100 * K)
        assert R0 + 104 * K <= nc.sbuf_usable_end, (R0, nc.sbuf_usable_end)
        XN = [sb(f"XN{n}", [P, 4, D], F32, R0 + off * K) for n, off in enumerate((40, 40, 40, 0))]

        PS = ctx.enter_context(nc.psum_tensor("PS", [P, 8, 512], F32))

        def bank(key):
            return J[key] % 8

        s_const = sem("consts_loaded")
        s_ident = sem("identity_loaded")
        s_c = sem("c_loaded")
        s_x = [sem(f"x_loaded_{b}") for b in range(B)]
        s_wm = [sem(f"wmod_loaded_{i}") for i in range(3)]
        s_wqkv = sem("wqkv_loaded")
        s_wo = sem("output_projection_loaded")
        s_l0w = sem("layer0_weights_loaded")
        s_rqf = sem("router_weights_loaded")
        s_w0p = sem("layer0_feedforward_weights_split")
        s_silu = sem("silu_c_ready")
        s_sct = sem("silu_c_padding_ready")
        s_mm = sem("jobs_multiplied")
        s_free = sem("banks_freed")
        s_cast = sem("jobs_rounded")
        s_whole = sem("modulated_inputs_ready")
        s_wqkvh = sem("wqkv_rounded")
        s_wqkvl = sem("wqkv_split")
        s_mc = sem("modulation_columns_ready")
        s_mr = sem("modulation_gates_ready")
        s_var = sem("variances_ready")
        s_sd = sem("deviations_ready")
        s_xn = sem("tiles_normalised")
        s_xnu = sem("tiles_transposed")
        s_ones = sem("attention_constants_ready")
        s_qks = [sem(f"qk_stack_loaded_{i}") for i in range(STACKS)]
        s_s = sem("scores_ready")
        s_mx = sem("row_maxima_ready")
        s_dg = sem("maxima_diagonal_ready")
        s_st = sem("transposed_scores_ready")
        s_exp = sem("exponentials_ready")
        s_pv = sem("values_weighted")
        s_ot = sem("head_outputs_copied")
        s_num = [sem(f"head_outputs_moved_{i}") for i in range(2)]
        s_last = [sem(f"last_outputs_moved_{h}") for h in range(REP)]
        s_rec = sem("last_sums_inverted")
        s_div1 = sem("last_heads_divided")
        s_oL1 = sem("last_heads_split")
        s_div = sem("heads_divided")
        s_oh = sem("heads_rounded")
        s_oL = sem("heads_split")
        s_w0h = sem("layer0_weights_rounded")
        s_w0l = sem("layer0_weights_split")
        s_nmx = sem("router_maxima_ready")
        s_ex = sem("router_exponentials_ready")
        s_code = [sem(f"codes_loaded_{i}") for i in range(2)]
        s_scale = [sem(f"scales_loaded_{i}") for i in range(2)]
        s_plane = sem("ramps_ready")
        s_used = sem("ramps_added")
        s_r0 = sem("first_ramps_ready")
        s_r0g = sem("first_ramps_ready_by_gpsimd")
        s_wf = sem("pieces_scaled")
        s_wh = sem("pieces_rounded")
        s_wl = sem("pieces_split")
        s_lora = [sem(f"lora_loaded_{i}") for i in range(3)]
        s_ldw = sem("lora_down_loaded")
        s_ph = sem("projection_weights_rounded")
        s_pl = sem("projection_weights_split")
        s_ll = sem("lora_weights_split")
        s_sg = sem("silu_ready")
        s_hsh = sem("hidden_rounded")
        s_hsl = sem("hidden_split")
        s_hsv = sem("hidden_split_by_vector")
        s_hsu = sem("hidden_used")
        s_out = sem("outputs_stored")
        s_ldh = sem("lora_down_rounded")
        s_x1 = sem("block_sums_ready")
        s_xadd = sem("results_added")
        s_x1u = sem("block_sums_added")
        s_ldl = sem("lora_down_split")
        ch_dve = sem("vector_chain")
        ch_pool = sem("gpsimd_chain")
        ch_act = sem("scalar_chain")

        class Chain:

            def __init__(self, eng, s):
                self.eng, self.s, self.n = eng, s, 0

            def __call__(self, ins):
                self.n += 1
                ins.then_inc(self.s, 1)
                self.eng.wait_ge(self.s, self.n)

        block = ctx.enter_context(nc.Block())
        GU_START = {0: GU0, 1: GU1}
        DN_START = {0: DN0, 1: DN1}
        HS_N = {0: 0, 1: MC}

        def slot(p):
            return (p - GU0) % RING

        def ring_no(p):
            return p - GU0 + 1

        def STC(n):
            return n * (TB * (TB + 1) // 2)

        def load_piece(sp, p):
            if p == GU0 + 2:
                sp.wait_ge(s_ll, 3)
                for q in (GU0, GU0 + 1):
                    sp.dma_start(WF[:, q % 2, PW:], a["LBGU"][q - GU0]).then_inc(s_scale[q % 2], 16)
            if p == 0:
                sp.wait_ge(s_mm, J["modrow", 1, 5] + 1)
            if p == N_QKV:
                sp.wait_ge(s_w0l, 1)
                sp.wait_ge(s_w0p, 3)
            if p >= 2:
                sp.wait_ge(s_plane, 7 * (p - 1))
                wait_first_ramp(sp, p - 2)
            sp.dma_start(CODE[:, p % 2], a["CODES"][p]).then_inc(s_code[p % 2], 16)
            if p >= 2:
                sp.wait_ge(s_wf, p - 1)
            for half in range(2):
                sp.dma_start(SCALE[64 * half:64 * half + 64, p % 2],
                             a["SCALES"][p, half:half + 1, :].to_broadcast([64, PW])).then_inc(s_scale[p % 2], 16)
            if GU0 + 2 <= p < DN0:
                sp.wait_ge(s_wl, ring_no(p) - 2)
                sp.dma_start(WF[:, p % 2, PW:], a["LBGU"][p - GU0]).then_inc(s_scale[p % 2], 16)

        def scale_loads(p):
            n = sum(2 + (GU0 <= q < DN0) for q in range(p % 2, p + 1, 2))
            return 16 * n

        def o_ramps(t):
            return [divmod(8 * N_QKV + 2 * t + i, 8) for i in range(2)]

        def projection_ramps(i):
            jobs_n = 2 * B * (KC + 1)
            first, last = (8 * AHEAD * x // jobs_n for x in (i, i + 1))
            return [divmod(8 * GU0 + step, 8) for step in range(first, last)]

        def load_stack(sp, n):
            b, g = divmod(n, GROUPS)
            if n == 0:
                sp.wait_ge(s_ones, 1)
            if g == 0:
                sp.wait_ge(s_free, J["k", b] + 1)
            if n >= STACKS:
                sp.wait_ge(s_st, STC(n - STACKS + 1))
            rows = slice(HD * g, HD * g + HD)
            cols = slice(b * S, b * S + S)
            for r, src in enumerate((FH, FH, FL, FL)):
                sp.dma_start(QS[HD * r:HD * r + HD, n % STACKS].bitcast(F32), src[rows, :, cols].bitcast(F32)
                             ).then_inc(s_qks[n % STACKS], 16)
            for r, src in enumerate((KH, KL, KH, KL)):
                sp.dma_start(KS[HD * r:HD * r + HD, n % STACKS].bitcast(F32), src[rows, cols].bitcast(F32)
                             ).then_inc(s_qks[n % STACKS], 16)

        def move_out(sp, n):
            b, g = divmod(n, GROUPS)
            sp.wait_ge(s_ot, n + 1)
            rows = slice(HD * g, HD * g + HD)
            cols = slice(b * S, b * S + S)
            for h in range(REP):
                moved = s_num[n % 2] if n < B * GROUPS - 1 else s_last[h]
                sp.dma_start(DEN[rows, h, cols], OT[32 * h + HD:32 * h + 32, n % 2]).then_inc(moved, 16)
                sp.dma_start(NUM[rows, h, cols], OT[32 * h:32 * h + HD, n % 2]).then_inc(moved, 16)

        def copy_heads(act, n):
            act.wait_ge(s_pv, TB * (n + 1))
            if n >= 2:
                act.wait_ge(s_num[n % 2], 128 * (n // 2))
            nc.scalar.activation(OT[:, n % 2], PS[:, 7], ACT.Copy).then_inc(s_ot, 1)


        def weights_used(eng, p):
            for n in range(2):
                if GU_START[n] <= p < DN_START[n]:
                    eng.wait_ge(s_mm, J["gu", n, p - GU_START[n], B - 1, 1] + 1)
                elif DN_START[n] <= p < DN_START[n] + MC // 2:
                    hidden_used(eng, n, 2 * (p - DN_START[n]) + 1)

        def hidden_used(eng, n, k):
            if k < MC - 1:
                eng.wait_ge(s_hsu, (MC - 1) * n + k + 1)
            else:
                eng.wait_ge(s_mm, J["down", n, NT - 1] + 1)

        def tile_transposed(eng, u):
            g, ti = divmod(u, TB)
            if ti < TB - 1:
                eng.wait_ge(s_xnu, (TB - 1) * g + ti + 1)
            else:
                eng.wait_ge(s_mm, J["norm", g // B, g % B, KC - 1] + 1)

        def ramp_by_gpsimd(p):
            return GU1 + AHEAD <= p < DN1 + AHEAD

        def wait_first_ramp(eng, p):
            same = [q for q in range(p + 1) if ramp_by_gpsimd(q) == ramp_by_gpsimd(p)]
            eng.wait_ge(s_r0g if ramp_by_gpsimd(p) else s_r0, len(same))

        def added(key):
            before = {"wo": 0, "y": 1, "down": 2 + key[1]}[key[0]]
            return NT * before + key[-1] + 1

        def by_vector(n, k):
            return n == 1 and k % 2 == 0

        def hidden_is_split(eng, n, k):
            if by_vector(n, k):
                eng.wait_ge(s_hsv, k // 2 + 1)
            else:
                eng.wait_ge(s_hsl, MC * n + k + 1 if n == 0 else MC + k // 2 + 1)

        @block.sync
        def _(sp):
            sp.dma_start(CT[:], a["CT"]).then_inc(s_c, 16)
            for l in range(2):
                for j in range(6):
                    n = 6 * l + j
                    if n == len(FIRST):
                        sp.dma_start(WQKVF[:, :, 0:D], a["WQ"].rearrange("(c p) n -> p c n", p=P)).then_inc(s_wqkv, 16)
                    if n >= 3:
                        key = ("modrow", (n - 3) // 6, (n - 3) % 6)
                        sp.wait_ge(s_mm, J[key] + 1)
                    sp.dma_start(WM[:, n % 3], a[f"WM{l}"].rearrange("(c p) n -> p c n", p=P)[:, :, j * D:(j + 1) * D]
                                 ).then_inc(s_wm[n % 3], 16)
            for n in range(B * GROUPS + STACKS):
                if n >= STACKS:
                    move_out(sp, n - STACKS)
                if n < B * GROUPS:
                    load_stack(sp, n)
                for p in PIECES_AT.get(n, ()):
                    load_piece(sp, p)
                if n == B * GROUPS + STACKS - 2:
                    sp.wait_ge(s_used, 7 * N_QKV)
                    sp.dma_start(WOF[:], a["WO"].rearrange("(c p) n -> p c n", p=P)).then_inc(s_wo, 16)
            sp.wait_ge(s_wf, N_QKV)
            for dst, name in ((ATF, "AT"), (BTF, "BT")):
                sp.dma_start(dst[:], a[name].rearrange("(c p) n -> p c n", p=P)).then_inc(s_l0w, 16)
            for p in range(N_QKV, PIECES):
                load_piece(sp, p)
            sp.wait_ge(s_out, 16 * NT)

        @block.gpsimd
        def _(pool):
            link = Chain(pool, ch_pool)
            nc.gpsimd.memset(SCT[:], 0.0).then_inc(s_sct, 1)
            pool.wait_ge(s_sct, 1)
            link(nc.gpsimd.memset(QS[64:P].rearrange("p a h s -> p (a h s)").bitcast(F32), 0.0))
            nc.gpsimd.memset(KS[64:P].rearrange("p a s -> p (a s)").bitcast(F32), 0.0).then_inc(s_ones, 1)
            pool.wait_ge(s_ones, 1)
            pool.wait_ge(s_ident, 16)
            pool.wait_ge(s_free, J["norm", 0, B - 1, KC - 1] + 1)
            link(nc.gpsimd.memset(V[:, :, :, 1, :], 1.0))
            def scale_piece(p):
                pool.wait_ge(s_used, 7 * (p + 1))
                pool.wait_ge(s_scale[p % 2], scale_loads(p))
                acc, sc = ACC[:, p % 2], SCALE[:, p % 2]
                if p < N_QKV:
                    if p < 2:
                        nc.gpsimd.tensor_tensor(WT[p][:], acc, sc, ALU.mult).then_inc(s_wf, 1)
                    else:
                        link(nc.gpsimd.tensor_tensor(acc, acc, sc, ALU.mult))
                elif p < GU0:
                    nc.gpsimd.tensor_tensor(acc, acc, sc, ALU.mult).then_inc(s_wf, 1)
                else:
                    if p < GU0 + 2:
                        pool.wait_ge(s_ll, 3)
                    else:
                        pool.wait_ge(s_wl, ring_no(p) - 2)
                    nc.gpsimd.tensor_tensor(WF[:, p % 2, 0:PW], acc, sc, ALU.mult).then_inc(s_wf, 1)

            def add_piece(p):
                if p < 2:
                    return
                pool.wait_ge(s_wf, p)
                if p >= 4:
                    for i in range(STACKS):
                        pool.wait_ge(s_qks[i], 128 * len(range(i, B * GROUPS, STACKS)))
                dst = WT[p % 2][:] if p < 4 else WSQ[:, p % 2]
                nc.gpsimd.tensor_tensor(dst, WT[p % 2][:], ACC[:, p % 2], ALU.add).then_inc(s_wf, 1)

            def add_gated(key):
                pool.wait_ge(s_free, J[key] + 1)
                nc.gpsimd.tensor_tensor(X[:, key[-1]], X[:, key[-1]], SCR[:, key[-1] % 2], ALU.add).then_inc(s_xadd, 1)

            last_ramp = [n for n in range(B * GROUPS * TB) if ramp_at(n) and ramp_at(n)[1] == 7]
            scale_at = {n + 1: p for p, n in enumerate(last_ramp)}
            add_at = {n + 2: p for p, n in enumerate(last_ramp)}
            del add_at[last_ramp[4] + 2]
            add_at[B * GROUPS * TB - 3] = 4
            for n in range(B * GROUPS * TB):
                pool.wait_ge(s_mx, 2 * n + 2)
                link(nc.gpsimd.tensor_scalar(MG[:, 0], MX[:, n % 2], 0.0, -2.0 ** -10, ALU.max, ALU.mult))
                link(nc.gpsimd.tensor_scalar(MG[:, 1], MX[:, n % 2], 2.0 ** -11 - 1.0, 0.0, ALU.mult, ALU.add))
                if n >= 1:
                    pool.wait_ge(s_dg, n)
                link(nc.gpsimd.tensor_tensor(MG[:, 2], MG[:, 0], MG[:, 1], ALU.add))
                if n >= 2:
                    done = STC((n - 2) // TB) + sum(i + 1 for i in range((n - 2) % TB + 1))
                    pool.wait_ge(s_st, done)
                nc.gpsimd.tensor_tensor(DG[:, n % 2], ident[:].unsqueeze(1).to_broadcast([P, REP, P]),
                                        MG[:, 2, :].unsqueeze(2).to_broadcast([P, REP, P]), ALU.mult
                                        ).then_inc(s_dg, 1)
                if n in scale_at:
                    scale_piece(scale_at[n])
                if n in add_at:
                    add_piece(add_at[n])
            pool.wait_ge(s_w0h, 1)
            nc.gpsimd.tensor_tensor(WOL[:], WOF[:], WOH[:], ALU.subtract).then_inc(s_w0l, 1)
            add_piece(N_QKV - 1)
            for h in range(REP + 1):
                if h < REP:
                    pool.wait_ge(s_rec, h + 1)
                    nc.gpsimd.tensor_tensor(NUM[:, h, S:], NUM[:, h, S:], DEN[:, h, S:], ALU.mult).then_inc(s_div1, 1)
                if h > 0:
                    pool.wait_ge(s_oh, REP + h)
                    nc.gpsimd.tensor_tensor(FL[:, h - 1, S:], NUM[:, h - 1, S:], FH[:, h - 1, S:], ALU.subtract
                                            ).then_inc(s_oL1, 1)
            for t in range(TB):
                add_gated(("wo", t))
            for i, (dst, raw, high) in enumerate(((RQL, RQF, RQH), (ATL, ATF, ATH), (BTL, BTF, BTH))):
                if i == 1:
                    for t in range(TB, NT):
                        add_gated(("wo", t))
                pool.wait_ge(s_w0h, i + 2)
                nc.gpsimd.tensor_tensor(dst[:], raw[:], high[:], ALU.subtract).then_inc(s_w0p, 1)
            pool.wait_ge(s_ph, 1)
            nc.gpsimd.tensor_tensor(WQL[:].rearrange("p c n -> p (c n)"), WSQ[:].rearrange("p a n -> p (a n)"),
                                    WQH[:].rearrange("p c n -> p (c n)"), ALU.subtract).then_inc(s_pl, 1)
            for t in range(NT):
                add_gated(("y", t))
                if t % TB == TB - 2:
                    scale_piece(N_QKV + t // TB)
            pool.wait_ge(s_ph, 3)
            nc.gpsimd.tensor_tensor(W2L[:].rearrange("p c n -> p (c n)"), ACC[:].rearrange("p a n -> p (a n)"),
                                    W2H[:].rearrange("p c n -> p (c n)"), ALU.subtract).then_inc(s_pl, 1)

            def split_piece(p):
                w = PW + (LBW if GU0 <= p < DN0 else 0)
                pool.wait_ge(s_wh, ring_no(p))
                nc.gpsimd.tensor_tensor(WRL[:, slot(p), 0:w], WF[:, p % 2, 0:w], WRH[:, slot(p), 0:w], ALU.subtract
                                        ).then_inc(s_wl, 1)

            def first_ramp(p):
                if p >= 2:
                    pool.wait_ge(s_wf, p - 1)
                pool.wait_ge(s_code[p % 2], 16 * (p // 2 + 1))
                nc.gpsimd.tensor_scalar(ACC[:, p % 2], CODE[:, p % 2], RAMP[0][0], RAMP[0][1], ALU.mult, ALU.add
                                        ).then_inc(s_r0g, 1)

            def step(p):
                if ramp_by_gpsimd(p + 1):
                    first_ramp(p + 1)
                if p < PIECES:
                    scale_piece(p)
                if GU0 <= p - 1 < PIECES:
                    split_piece(p - 1)

            def hidden_split(n, k):
                i = HS_N[n] + k
                pool.wait_ge(s_hsh, i + 1)
                nc.gpsimd.tensor_tensor(HL[:, k % 4], HID[:, k], HH[:, k % 4], ALU.subtract).then_inc(s_hsl, 1)

            for p in range(GU0, GU0 + AHEAD):
                step(p)
            for n in range(2):
                for m in range(MC - 1):
                    step(GU_START[n] + m + AHEAD)
                for k in range(2):
                    if not by_vector(n, k):
                        hidden_split(n, k)
                step(DN_START[n] - 1 + AHEAD)
                for i in range(MC // 2):
                    for k in (2 * i + 2, 2 * i + 3):
                        if k < MC and not by_vector(n, k):
                            hidden_split(n, k)
                    step(DN_START[n] + i + AHEAD)
                for t in range(NT):
                    add_gated(("down", n, t))

        @block.scalar
        def _(act):
            act.dma_start(ident[:], a["IDENT"]).then_inc(s_ident, 16)
            for b in range(B):
                act.dma_start(X[:, b * TB:(b + 1) * TB], a["X"].rearrange("(t p) d -> p t d", p=P)[:, b * TB:(b + 1) * TB]
                              ).then_inc(s_x[b], 16)
            for dst, name in ((identB, "IDENTB"), (maskB, "MASKB"), (sel, "SEL"), (sumsel, "SUMSEL")):
                act.dma_start(dst[:], a[name]).then_inc(s_const, 16)
            act.dma_start(WQKVF[:, :, D:D + KVW], a["WK"].rearrange("(c p) n -> p c n", p=P)).then_inc(s_wqkv, 16)
            act.dma_start(WQKVF[:, :, D + KVW:], a["WV"].rearrange("(c p) n -> p c n", p=P)).then_inc(s_wqkv, 16)
            act.wait_ge(s_c, 16)
            act.wait_ge(s_sct, 1)
            nc.scalar.activation(SCT[:, :, :, 0:B], CT[:], ACT.Silu).then_inc(s_silu, 1)
            act.wait_ge(s_ident, 16)
            nc.scalar.activation(identR[:], ident[:], ACT.Copy).then_inc(s_silu, 1)
            nc.scalar.activation(onesR[:], ident[:], ACT.Identity, scale=0.0, bias=1.0).then_inc(s_silu, 1)

            def deviations(n, b):
                act.wait_ge(s_var, 2 * n + b + 1)
                tiles = slice(b * TB, (b + 1) * TB)
                nc.scalar.activation(SD[:, tiles], MV[:, tiles, 1], ACT.Sqrt, bias=EPS).then_inc(s_sd, 1)

            def norm_round(n, b):
                layer, v = divmod(n, 2)
                for c in range(KC):
                    if (b, c) == (0, 0):
                        act.wait_ge(s_mc, n + 1)
                    act.wait_ge(s_mm, J["norm", n, b, c] + 1)
                    for dst, done in ((HH[:, c, b * S:(b + 1) * S], s_cast), (XN[n][:, 2], s_whole)):
                        if done is s_whole:
                            if c % 2:
                                break
                            act.wait_ge(s_free, J["norm", n, b, c] - 1)
                        nc.scalar.activation(dst, PS[:, bank(("norm", n, b, c))], ACT.Identity,
                                             scale=MCOL[:, layer, 2 * v + 1, c, b:b + 1],
                                             bias=MCOL[:, layer, 2 * v, c, b:b + 1]).then_inc(done, 1)

            def norm(n):
                for b in range(B):
                    deviations(n, b)
                    norm_round(n, b)

            for b in range(B):
                deviations(0, b)
            norm_round(0, 0)
            act.wait_ge(s_wqkv, 48)
            nc.scalar.activation(WQKVH[:], WQKVF[:], ACT.Copy).then_inc(s_wqkvh, 1)
            norm_round(0, 1)
            for b in range(B):
                cols = slice(b * S, (b + 1) * S)
                for h in range(REP):
                    act.wait_ge(s_mm, J["q", b, h] + 1)
                    nc.scalar.activation(FH[:, h, cols], PS[:, bank(("q", b, h))], ACT.Copy).then_inc(s_cast, 1)
                act.wait_ge(s_mm, J["k", b] + 1)
                nc.scalar.activation(KH[:, cols], PS[:, bank(("k", b))], ACT.Copy).then_inc(s_cast, 1)
            def plane(p, i):
                n = 7 * p + i
                if i == 0:
                    act.wait_ge(s_code[p % 2], 16 * (p // 2 + 1))
                if n >= 3:
                    act.wait_ge(s_used, n - 2)
                r = PLANES[i]
                nc.scalar.activation(PL[:, n % 3], CODE[:, p % 2], ACT.Relu, scale=RAMP[r][0], bias=RAMP[r][1]
                                     ).then_inc(s_plane, 1)

            def planes(p):
                for i in range(7):
                    plane(p, i)

            def round_heads(b, h):
                act.wait_ge(s_div1 if b else s_div, h + 1)
                nc.scalar.activation(FH[:, h, b * S:(b + 1) * S], NUM[:, h, b * S:(b + 1) * S], ACT.Copy
                                     ).then_inc(s_oh, 1)

            def ride(n):
                if ramp_at(n) and ramp_at(n)[1] > 0:
                    plane(ramp_at(n)[0], ramp_at(n)[1] - 1)

            for n in range(3):
                ride(n)
            act.wait_ge(s_free, J["gsum",] + 1)
            done = 0
            for n in range(B * GROUPS * TB):
                ic = n % TB
                if n >= 2:
                    act.wait_ge(s_pv, n - 1)
                for jc in range(ic + 1):
                    act.wait_ge(s_st, done + 1)
                    nc.scalar.activation(PT[:, n % 2, jc].rearrange("p h i -> p (h i)"), PS[:, 4 + done % 3],
                                         ACT.Exp, scale=HD ** -0.5).then_inc(s_exp, 1)
                    done += 1
                if ic == 0 and n:
                    copy_heads(act, n // TB - 1)
                ride(n + 3)
                if n in HEADS0_AT:
                    round_heads(0, HEADS0_AT.index(n))
            copy_heads(act, B * GROUPS - 1)
            act.wait_ge(s_wo, 16)
            act.wait_ge(s_pv, B * GROUPS * TB)
            nc.scalar.activation(WOH[:], WOF[:], ACT.Copy).then_inc(s_w0h, 1)
            for h in range(REP):
                round_heads(1, h)
            for h in range(REP):
                act.wait_ge(s_last[h], 32)
            act.dma_start(LDA[:], a["LDA"]).then_inc(s_ldw, 16)
            act.wait_ge(s_wf, N_QKV)
            act.dma_start(RQF[:], a["RQ"]).then_inc(s_rqf, 16)
            act.dma_start(KEYS[:], a["KEYS"]).then_inc(s_rqf, 16)
            act.wait_ge(s_rqf, 32)
            nc.scalar.activation(RQH[:], RQF[:], ACT.Copy).then_inc(s_w0h, 1)
            act.wait_ge(s_l0w, 32)
            nc.scalar.activation(ATH[:], ATF[:], ACT.Copy).then_inc(s_w0h, 1)
            nc.scalar.activation(BTH[:], BTF[:], ACT.Copy).then_inc(s_w0h, 1)
            norm(1)
            act.wait_ge(s_mm, J["wo", NT - 1] + 1)
            act.wait_ge(s_wf, N_QKV)
            nc.scalar.activation(WQH[:].rearrange("p c n -> p (c n)"), WSQ[:].rearrange("p a n -> p (a n)"),
                                 ACT.Copy).then_inc(s_ph, 1)
            for t in range(NT):
                act.wait_ge(s_nmx, t + 1)
                nc.scalar.activation(EX[:, t], SCO[:, t], ACT.Exp, bias=NMX[:, t:t + 1]).then_inc(s_ex, 1)
            act.wait_ge(s_mm, J["rq", B - 1] + 1)
            act.dma_start(LF[:], a["LQKV"]).then_inc(s_lora[0], 16)
            act.wait_ge(s_pl, 1)

            def round_piece(p):
                w = PW + (LBW if GU0 <= p < DN0 else 0)
                act.wait_ge(s_wf, p + 1)
                if GU0 <= p < DN0:
                    act.wait_ge(s_scale[p % 2], scale_loads(p))
                if p < GU0 + RING:
                    if p == GU0:
                        act.wait_ge(s_mm, J["o", B - 1, KC - 1] + 1)
                else:
                    weights_used(act, p - RING)
                nc.scalar.activation(WRH[:, slot(p), 0:w], WF[:, p % 2, 0:w], ACT.Copy).then_inc(s_wh, 1)

            for t in range(NT):
                act.wait_ge(s_mm, J["zt", t] + 1)
                nc.scalar.activation(FH[:, :, t * P:(t + 1) * P],
                                     PS[:, bank(("zt", t))].rearrange("p (c k) -> p c k", c=KC), ACT.Copy
                                     ).then_inc(s_cast, 1)
                for p, i in o_ramps(t):
                    if i > 0:
                        plane(p, i - 1)
                if t == 1:
                    act.wait_ge(s_lora[0], 16)
                    nc.scalar.activation(LQ[:, 0], LF[:], ACT.Copy).then_inc(s_ph, 1)
                if t == NT - 2:
                    deviations(2, 0)
            deviations(2, 1)
            act.wait_ge(s_mm, J["z", NT - 1] + 1)
            act.wait_ge(s_wf, GU0)
            nc.scalar.activation(W2H[:].rearrange("p c n -> p (c n)"), ACC[:].rearrange("p a n -> p (a n)"),
                                 ACT.Copy).then_inc(s_ph, 1)
            act.wait_ge(s_ll, 1)
            act.dma_start(LF[:], a["LO"]).then_inc(s_lora[1], 16)
            for b in range(B):
                norm_round(2, b)
            def round_inner(key):
                act.wait_ge(s_mm, J[key] + 1)
                nc.scalar.activation(TL[:, key[1] * S:(key[1] + 1) * S], PS[:, bank(key)], ACT.Copy).then_inc(s_cast, 1)

            def ride(i):
                for p, step in projection_ramps(i):
                    if step > 0:
                        plane(p, step - 1)

            for b in range(B):
                cols = slice(b * S, (b + 1) * S)
                round_inner(("tqkv", b))
                ride(b * (KC + 1))
                for m in range(KC):
                    act.wait_ge(s_mm, J["qkv", b, m] + 1)
                    nc.scalar.activation(FH[:, m, cols], PS[:, bank(("qkv", b, m))], ACT.Copy, scale=1.0 / 3.0
                                         ).then_inc(s_cast, 1)
                    ride(b * (KC + 1) + m + 1)
                if b == 0:
                    act.wait_ge(s_lora[1], 16)
                    nc.scalar.activation(LOA[:, 0], LF[:, 0:KC * P], ACT.Copy).then_inc(ch_act, 1)
                    nc.scalar.activation(LOB[:, 0], LF[:, KC * P:], ACT.Copy).then_inc(s_ph, 1)
                    act.wait_ge(s_ll, 2)
                    act.dma_start(LF[:, 0:KC * P], a["LGA"]).then_inc(s_lora[2], 16)
            act.wait_ge(s_lora[2], 16)
            nc.scalar.activation(LGA[:, 0], LF[:, 0:KC * P], ACT.Copy).then_inc(s_ph, 1)
            for b in range(B):
                cols = slice(b * S, (b + 1) * S)
                round_inner(("to", b))
                ride((B + b) * (KC + 1))
                for m in range(KC):
                    act.wait_ge(s_x1, b * KC + m + 1)
                    nc.scalar.activation(HH[:, m, cols], X1T[:], ACT.Copy).then_inc(s_cast, 1)
                    ride((B + b) * (KC + 1) + m + 1)

            def step(p):
                if GU0 + AHEAD <= p < PIECES:
                    planes(p)
                if GU0 <= p - 1 < PIECES:
                    round_piece(p - 1)

            def round_hidden(n, k):
                i = HS_N[n] + k
                if k < 4:
                    act.wait_ge(s_mm, J["gu", n, MC - 1, B - 1, 1] + 1)
                    if n == 0:
                        act.wait_ge(s_x1u, k + 1)
                else:
                    hidden_used(act, n, k - 4)
                act.wait_ge(s_free, J["gu", n, k, B - 1, 1] + 1)
                nc.scalar.activation(HH[:, k % 4], HID[:, k], ACT.Copy).then_inc(s_hsh, 1)

            for p in range(GU0, GU0 + AHEAD):
                step(p)
            for b in range(B):
                round_inner(("tgu", b))
            act.wait_ge(s_mm, J["tgu", B - 1] + 1)
            act.wait_ge(s_ll, 3)
            act.dma_start(LDBF[:], a["LDB"]).then_inc(s_ldw, 16)
            for n in range(2):
                for m in range(MC):
                    p = GU_START[n] + m + AHEAD
                    if m < MC - 1:
                        step(p)
                    else:
                        for i in range(HALF):
                            plane(p, i)
                    for b in range(B):
                        i = (n * MC + m) * B + b
                        act.wait_ge(s_mm, J["gu", n, m, b, 0] + 1)
                        if i >= 2:
                            bn, mn, nn = (i - 2) % B, (i - 2) // B % MC, (i - 2) // B // MC
                            act.wait_ge(s_free, J["gu", nn, mn, bn, 1] + 1)
                        nc.scalar.activation(SG[:, i % 2], PS[:, bank(("gu", n, m, b, 0))], ACT.Silu).then_inc(s_sg, 1)
                if n == 0:
                    for i in range(HALF, 7):
                        plane(p, i)
                    round_piece(p - 1)
                    act.wait_ge(s_ldw, 32)
                    nc.scalar.activation(LDBH[:], LDBF[:], ACT.Copy).then_inc(s_ldh, 1)
                    for b in range(B):
                        act.wait_ge(s_mm, J["td", b] + 1)
                        nc.scalar.activation(TDH[:, b * S:(b + 1) * S], PS[:, bank(("td", b))], ACT.Copy
                                             ).then_inc(s_cast, 1)
                for k in range(2):
                    round_hidden(n, k)
                if n == 1:
                    for i in range(HALF, 7):
                        plane(p, i)
                    round_piece(p - 1)
                for i in range(MC // 2):
                    if 2 * i + 2 < MC:
                        round_hidden(n, 2 * i + 2)
                        round_hidden(n, 2 * i + 3)
                    step(DN_START[n] + i + AHEAD)
                if n == 0:
                    norm(3)
            for t in range(NT):
                act.wait_ge(s_xadd, added(("down", 1, t)))
                act.dma_start(out.rearrange("(t p) d -> t p d", p=P)[t], X[:, t]).then_inc(s_out, 16)

        @block.vector
        def _(dve):
            link = Chain(dve, ch_dve)

            def mod_row(l, j):
                dst = MRT[:, COLS.index(j) % 2] if j in COLS else MRG[:, 2 * l + j // 3]
                dve.wait_ge(s_mm, J["modrow", l, j] + 1)
                if j in COLS and (l, j) not in ((0, 0), (0, 1)):
                    before = 4 * l + COLS.index(j) - 2
                    dve.wait_ge(s_mm, J["modcol", before // 4, COLS[before % 4]] + 1)
                nc.vector.tensor_copy(dst, PS[:, bank(("modrow", l, j))]).then_inc(s_free, 1)

            def mod_column(l, j):
                v = COLS.index(j)
                dve.wait_ge(s_mm, J["modcol", l, j] + 1)
                nc.vector.reduce_sum(MCOL[:, l, v],
                                     PS[:, bank(("modcol", l, j))].rearrange("p (c k m) -> p c m k", k=KC, m=32)
                                     [:, :, 0:B, :], AX_X).then_inc(s_free, 1)
                if v % 2:
                    dve.wait_ge(s_free, J["modcol", l, j] + 1)
                    nc.vector.tensor_scalar(MCOL[:, l, v], MCOL[:, l, v], 1.0, None, ALU.add).then_inc(s_mc, 1)

            def gate_values():
                dve.wait_ge(s_free, J["gsum",] + 1)
                link(nc.vector.tensor_scalar(MR[:], GR[:], 0.0, 2.0, ALU.is_ge, ALU.mult))
                link(nc.vector.scalar_tensor_tensor(GR[:], GR[:], -1.0, GR[:], ALU.mult, ALU.max))
                link(nc.vector.tensor_scalar(GR[:], GR[:], 0.25, None, ALU.max))
                nc.vector.scalar_tensor_tensor(MR[:], MR[:], -1.0, GR[:], ALU.add, ALU.mult).then_inc(s_mr, 1)

            def stats(t):
                link(nc.vector.bn_stats(ST6[:, t], X[:, t]))
                ins = nc.vector.bn_aggr(MV[:, t], ST6[:, t])
                if t % TB == TB - 1:
                    ins.then_inc(s_var, 1)
                else:
                    link(ins)

            def normalise(n, b):
                dve.wait_ge(s_sd, B * n + b + 1)
                link(nc.vector.reciprocal(RS[:, b * TB:(b + 1) * TB], SD[:, b * TB:(b + 1) * TB]))
                for ti in range(TB):
                    t = b * TB + ti
                    u = (B * n + b) * TB + ti
                    if u % (B * TB) >= 2:
                        tile_transposed(dve, u - 2)
                    nc.vector.tensor_scalar(XN[n][:, u % 2], X[:, t], MV[:, t, 0:1], RS[:, t:t + 1],
                                            ALU.subtract, ALU.mult).then_inc(s_xn, 1)

            def modulate(n, b):
                layer, v = divmod(n, 2)
                for c in range(KC):
                    key = ("norm", n, b, c)
                    cols = slice(b * S, (b + 1) * S)
                    dve.wait_ge(s_cast, CAST[key])
                    if c % 2:
                        dve.wait_ge(s_free, J[key] - 1)
                        link(nc.vector.tensor_scalar(XN[n][:, 3], PS[:, bank(key)], MCOL[:, layer, 2 * v + 1, c, b:b + 1],
                                                     MCOL[:, layer, 2 * v, c, b:b + 1], ALU.mult, ALU.add))
                    else:
                        dve.wait_ge(s_whole, ((B * n + b) * KC + c) // 2 + 1)
                    nc.vector.tensor_tensor(HL[:, c, cols], XN[n][:, 2 + c % 2], HH[:, c, cols], ALU.subtract
                                            ).then_inc(s_free, 1)

            def rest(dst, key, high, scale=None, rows=slice(0, P)):
                dve.wait_ge(s_mm, J[key] + 1)
                dve.wait_ge(s_cast, CAST[key])
                src = PS[rows, bank(key)]
                if scale is None:
                    ins = nc.vector.tensor_tensor(dst, src, high, ALU.subtract)
                else:
                    ins = nc.vector.scalar_tensor_tensor(dst, src, scale, high, ALU.mult, ALU.subtract)
                ins.then_inc(s_free, 1)

            def gates(name):
                for b in range(B):
                    dve.wait_ge(s_mm, J[name, b] + 1)
                    nc.vector.tensor_copy(GAB[:, b], PS[:, bank((name, b))]).then_inc(s_free, 1)
                dve.wait_ge(s_free, J[name, B - 1] + 1)

            def gated(key):
                t = key[-1]
                dve.wait_ge(s_mm, J[key] + 1)
                if added(key) > 2:
                    dve.wait_ge(s_xadd, added(key) - 2)
                nc.vector.tensor_tensor(SCR[:, t % 2], PS[:, bank(key)], GAB[:, t // TB], ALU.mult).then_inc(s_free, 1)

            def ramp(p, i):
                acc = ACC[:, p % 2]
                if i == 0:
                    if ramp_by_gpsimd(p):
                        return
                    dve.wait_ge(s_code[p % 2], 16 * (p // 2 + 1))
                    if p >= 2:
                        dve.wait_ge(s_wf, p - 1)
                    if p == GU0:
                        dve.wait_ge(s_pl, 2)
                    nc.vector.tensor_scalar(acc, CODE[:, p % 2], RAMP[0][0], RAMP[0][1], ALU.mult, ALU.add
                                            ).then_inc(s_r0, 1)
                    return
                n, r = 7 * p + i - 1, PLANES[i - 1]
                dve.wait_ge(s_plane, n + 1)
                if i == 1:
                    wait_first_ramp(dve, p)
                    ins = nc.vector.scalar_tensor_tensor(acc, acc, RAMP[0][2], PL[:, n % 3], ALU.min, ALU.add)
                else:
                    dve.wait_ge(s_used, n)
                    ins = nc.vector.scalar_tensor_tensor(acc, PL[:, n % 3], RAMP[r][2], acc, ALU.min, ALU.add)
                ins.then_inc(s_used, 1)

            def hidden_split(n, k):
                dve.wait_ge(s_hsh, HS_N[n] + k + 1)
                nc.vector.tensor_tensor(HL[:, k % 4], HID[:, k], HH[:, k % 4], ALU.subtract).then_inc(s_hsv, 1)

            def decode(p):
                for i in range(8):
                    ramp(p, i)

            def divide(h):
                cols = slice(0, S)
                for i in range(2):
                    dve.wait_ge(s_num[i], 512)
                link(nc.vector.reciprocal(DEN[:, h, cols], DEN[:, h, cols]))
                nc.vector.tensor_tensor(NUM[:, h, cols], NUM[:, h, cols], DEN[:, h, cols], ALU.mult).then_inc(s_div, 1)

            def split_heads(h):
                cols = slice(0, S)
                dve.wait_ge(s_oh, h + 1)
                nc.vector.tensor_tensor(FL[:, h, cols], NUM[:, h, cols], FH[:, h, cols], ALU.subtract).then_inc(s_oL, 1)

            for b in range(B):
                dve.wait_ge(s_x[b], 16)
                for ti in range(TB):
                    stats(b * TB + ti)
                if b == 0:
                    for j in FIRST:
                        mod_row(0, j)
                    for j in FIRST:
                        mod_column(0, j)
                normalise(0, b)
            modulate(0, 0)
            dve.wait_ge(s_wqkvh, 1)
            nc.vector.tensor_tensor(WQKVL[:], WQKVF[:], WQKVH[:], ALU.subtract).then_inc(s_wqkvl, 1)
            modulate(0, 1)
            for i, key in enumerate(PROJECTIONS):
                b = key[1]
                cols = slice(b * S, (b + 1) * S)
                if key[0] == "q":
                    rest(FL[:, key[2], cols], key, FH[:, key[2], cols])
                elif key[0] == "k":
                    rest(KL[:, cols], key, KH[:, cols])
                elif key[0] == "vt":
                    dve.wait_ge(s_mm, J[key] + 1)
                    if b:
                        dve.wait_ge(s_mm, J["v", b - 1] + 1)
                    nc.vector.tensor_copy(VT[:], PS[:, bank(key)]).then_inc(s_free, 1)
                else:
                    dve.wait_ge(s_mm, J[key] + 1)
                    nc.vector.tensor_copy(V[:, b * TB:(b + 1) * TB, :, 0, :],
                                          PS[:, bank(key)].rearrange("p (t g d) -> p t g d", t=TB, g=GROUPS)
                                          ).then_inc(s_free, 1)
                for row in row_after(i):
                    mod_row(*row)
                for row in column_after(i):
                    mod_column(*row)
            dve.wait_ge(s_mm, J["gsum",] + 1)
            nc.vector.tensor_copy(GR[:], PS[:, bank(("gsum",))]).then_inc(s_free, 1)
            for n in range(B * GROUPS * TB):
                for pair in range(2):
                    dve.wait_ge(s_s, 2 * n + pair + 1)
                    if n >= 2:
                        dve.wait_ge(s_dg, n - 1)
                    w = (n % TB + 1) * P
                    nc.vector.reduce_max(MX[:, n % 2, 2 * pair:2 * pair + 2], PS[:, 2 * pair:2 * pair + 2, 0:w], AX_X
                                         ).then_inc(s_mx, 1)
                if ramp_at(n):
                    ramp(*ramp_at(n))
                if n == TB - 1:
                    gate_values()
                if n in HEADS0_AT:
                    h = HEADS0_AT.index(n)
                    divide(h)
                    if h > 0:
                        split_heads(h - 1)
                if n == HEADS0_AT[-1] + 4:
                    split_heads(REP - 1)
            dve.wait_ge(s_num[0], 64 * B * GROUPS)
            dve.wait_ge(s_num[1], 64 * B * GROUPS - 128)
            for h in range(REP):
                dve.wait_ge(s_last[h], 32)
                nc.vector.reciprocal(DEN[:, h, S:], DEN[:, h, S:]).then_inc(s_rec, 1)
            gates("ga0")
            gated(("wo", 0))
            for b in range(B):
                for ti in range(TB):
                    t = b * TB + ti
                    if t + 1 < NT:
                        gated(("wo", t + 1))
                    dve.wait_ge(s_xadd, added(("wo", t)))
                    stats(t)
                if b:
                    modulate(1, b - 1)
                normalise(1, b)
            modulate(1, B - 1)
            for b in range(B):
                dve.wait_ge(s_mm, J["rq", b] + 1)
                nc.vector.tensor_copy(RQ[:, b * S:(b + 1) * S], PS[0:ROUTER, bank(("rq", b))]).then_inc(s_free, 1)
            for b in range(B):
                dve.wait_ge(s_mm, J["score", b] + 1)
                nc.vector.tensor_copy(SCO[:, b * TB:(b + 1) * TB].rearrange("p t e -> p (t e)"),
                                      PS[:, bank(("score", b)), 0:TB * EXPERTS]).then_inc(s_free, 1)
            dve.wait_ge(s_free, J["score", B - 1] + 1)
            for t in range(NT):
                link(nc.vector.max(T8[:, t, 0], SCO[:, t]))
                nc.vector.tensor_scalar(NMX[:, t:t + 1], T8[:, t, 0, 0:1], -1.0, None, ALU.mult).then_inc(s_nmx, 1)
                link(nc.vector.match_replace(SC1[:, t], T8[:, t, 0], SCO[:, t], -3e38))
                link(nc.vector.max(T8[:, t, 1], SC1[:, t]))
                link(nc.vector.match_replace(SC2[:, t], T8[:, t, 1], SC1[:, t], -3e38))
            link(nc.vector.tensor_tensor(SC1[:], SC2[:], SCO[:], ALU.not_equal))
            dve.wait_ge(s_ex, NT)
            link(nc.vector.tensor_tensor(EX[:], EX[:], SC1[:], ALU.mult))
            link(nc.vector.reduce_sum(SUM[:], EX[:], AX_X))
            link(nc.vector.reciprocal(RSUM[:], SUM[:]))
            link(nc.vector.tensor_scalar(RSUM[:], RSUM[:], ALPHA / TOPK, None, ALU.mult))
            link(nc.vector.tensor_tensor(GATE[:], EX[:], RSUM[:].unsqueeze(2).to_broadcast([P, NT, EXPERTS]), ALU.mult))
            gates("gb0")
            for i in range(NT + LAG + 1):
                if i < NT:
                    if i >= 4:
                        dve.wait_ge(s_mm, J["zt", i - 4] + 1)
                    dve.wait_ge(s_mm, J["z", i] + 1)
                    nc.vector.tensor_tensor(XN[1][:, i % 4].rearrange("p (e r) -> p e r", r=RANK),
                                            PS[:, bank(("z", i))].rearrange("p (e r) -> p e r", r=RANK),
                                            GATE[:, i].unsqueeze(2).to_broadcast([P, EXPERTS, RANK]), ALU.mult
                                            ).then_inc(s_free, 1)
                if 0 <= i - LAG < NT:
                    t = i - LAG
                    cols = slice(t * P, (t + 1) * P)
                    dve.wait_ge(s_mm, J["zt", t] + 1)
                    dve.wait_ge(s_cast, CAST["zt", t])
                    nc.vector.tensor_tensor(FL[:, :, cols], PS[:, bank(("zt", t))].rearrange("p (c k) -> p c k", c=KC),
                                            FH[:, :, cols], ALU.subtract).then_inc(s_free, 1)
                if i > LAG:
                    gated(("y", i - LAG - 1))
                if i > LAG + 1:
                    t = i - LAG - 2
                    dve.wait_ge(s_xadd, added(("y", t)))
                    stats(t)
                if 0 <= i - LAG < NT:
                    for p, step in o_ramps(i - LAG):
                        ramp(p, step)
                if i == LAG + 2:
                    dve.wait_ge(s_ph, 2)
                    nc.vector.tensor_tensor(LQ[:, 1], LF[:], LQ[:, 0], ALU.subtract).then_inc(s_ll, 1)
            dve.wait_ge(s_xadd, added(("y", NT - 1)))
            stats(NT - 1)
            for b in range(B):
                normalise(2, b)
            for b in range(B):
                modulate(2, b)
            def inner(key):
                cols = slice(key[1] * S, (key[1] + 1) * S)
                rest(TL[64:P, cols], key, TL[64:P, cols], rows=slice(64, P))

            def ride(i):
                for p, step in projection_ramps(i):
                    ramp(p, step)

            for b in range(B):
                inner(("tqkv", b))
                ride(b * (KC + 1))
                for m in range(KC):
                    cols = slice(b * S, (b + 1) * S)
                    rest(FL[:, m, cols], ("qkv", b, m), FH[:, m, cols], scale=1.0 / 3.0)
                    ride(b * (KC + 1) + m + 1)
                if b == 0:
                    dve.wait_ge(s_ph, 4)
                    dve.wait_ge(ch_act, 1)
                    link(nc.vector.tensor_tensor(LOA[:, 1], LF[:, 0:KC * P], LOA[:, 0], ALU.subtract))
                    nc.vector.tensor_tensor(LOB[:, 1], LF[:, KC * P:], LOB[:, 0], ALU.subtract).then_inc(s_ll, 1)
            dve.wait_ge(s_ph, 5)
            nc.vector.tensor_tensor(LGA[:, 1], LF[:, 0:KC * P], LGA[:, 0], ALU.subtract).then_inc(s_ll, 1)
            for b in range(B):
                inner(("to", b))
                ride((B + b) * (KC + 1))
                for m in range(KC):
                    key, cols = ("o", b, m), slice(b * S, (b + 1) * S)
                    dve.wait_ge(s_mm, J[key] + 1)
                    link(nc.vector.tensor_tensor(X1T[:], PS[:, bank(key)], HH[:, m, cols], ALU.add))
                    nc.vector.tensor_tensor(X1T[:], X1T[:], HL[:, m, cols], ALU.add).then_inc(s_x1, 1)
                    dve.wait_ge(s_cast, CAST[key])
                    nc.vector.tensor_tensor(HL[:, m, cols], X1T[:], HH[:, m, cols], ALU.subtract).then_inc(s_free, 1)
                    dve.wait_ge(s_free, J[key] + 1)
                    ride((B + b) * (KC + 1) + m + 1)
            for b in range(B):
                inner(("tgu", b))
            for n in range(2):
                for m in range(MC):
                    p = GU_START[n] + m + AHEAD
                    for i in range(8 if m < MC - 1 else HALF + 1):
                        ramp(p, i)
                    for b in range(B):
                        i = (n * MC + m) * B + b
                        dve.wait_ge(s_mm, J["gu", n, m, b, 1] + 1)
                        dve.wait_ge(s_sg, i + 1)
                        nc.vector.tensor_tensor(HID[:, m, b * S:(b + 1) * S], SG[:, i % 2],
                                                PS[:, bank(("gu", n, m, b, 1))], ALU.mult).then_inc(s_free, 2)
                if n == 0:
                    dve.wait_ge(s_ldh, 1)
                    nc.vector.tensor_tensor(LDBL[:], LDBF[:], LDBH[:], ALU.subtract).then_inc(s_ldl, 1)
                    for b in range(B):
                        cols = slice(b * S, (b + 1) * S)
                        rest(TDL[:, cols], ("td", b), TDH[:, cols])
                if n == 0:
                    gates(f"g{n}")
                else:
                    hidden_split(n, 0)
                for i in range(HALF + 1, 8):
                    ramp(p, i)
                if n == 1:
                    gates(f"g{n}")
                for i in range(MC // 2):
                    if n == 1 and 2 * i + 2 < MC:
                        hidden_split(n, 2 * i + 2)
                    if DN_START[n] + i + AHEAD < PIECES:
                        decode(DN_START[n] + i + AHEAD)
                gated(("down", n, 0))
                for b in range(B):
                    for ti in range(TB):
                        t = b * TB + ti
                        if t + 1 < NT:
                            gated(("down", n, t + 1))
                        if n == 0:
                            dve.wait_ge(s_xadd, added(("down", n, t)))
                            stats(t)
                    if n == 0:
                        if b:
                            modulate(3, b - 1)
                        normalise(3, b)
                if n == 0:
                    modulate(3, B - 1)

        @block.tensor
        def _(pe):
            def begin(key):
                if J[key] >= 8:
                    pe.wait_ge(s_free, J[key] - 7)
                return PS[:, bank(key)]

            def product(dst, left, right, start=True, stop=True):
                pairs = [(left(k), right(k)) for k in range(KC)]
                for k, ((lh, ll), (rh, rl)) in enumerate(pairs):
                    nc.tensor.matmul(dst, lh, rh, start=start and k == 0, stop=False)
                    nc.tensor.matmul(dst, ll, rh, start=False, stop=False)
                    ins = nc.tensor.matmul(dst, lh, rl, start=False, stop=stop and k == KC - 1)
                return ins

            def h_cols(cols):
                return lambda k: (HH[:, k, cols], HL[:, k, cols])

            def f_cols(cols):
                return lambda k: (FH[:, k, cols], FL[:, k, cols])

            def pair(hi, lo, cols):
                return lambda k: (hi[:, k, cols], lo[:, k, cols])

            def mod_row(l, j):
                n = 6 * l + j
                if n == 0:
                    pe.wait_ge(s_silu, 1)
                dst = begin(("modrow", l, j))
                pe.wait_ge(s_wm[n % 3], 16 * (n // 3 + 1))
                for k in range(KC):
                    q = 32 * k
                    ins = nc.tensor.matmul(dst[q:q + 32], SCT[:, l, k], WM[:, n % 3, k], start=True, stop=True,
                                           tile_position=(0, q))
                ins.then_inc(s_mm, 1)

            def mod_column(l, j):
                dst = begin(("modcol", l, j))
                pe.wait_ge(s_free, J["modrow", l, j] + 1)
                for c in range(KC):
                    ins = nc.tensor.transpose(dst[:, c * P:(c + 1) * P],
                                              MRT[:, COLS.index(j) % 2, c * P:(c + 1) * P], ident[:])
                ins.then_inc(s_mm, 1)

            def norm(n):
                for b in range(B):
                    dst = [begin(("norm", n, b, c)) for c in range(KC)]
                    for ti in range(TB):
                        u = (B * n + b) * TB + ti
                        pe.wait_ge(s_xn, u + 1)
                        for c in range(KC):
                            ins = nc.tensor.transpose(dst[c][:, ti * P:(ti + 1) * P],
                                                      XN[n][:, u % 2, c * P:(c + 1) * P], ident[:])
                            if ti == TB - 1:
                                ins.then_inc(s_mm, 1)
                        if ti < TB - 1:
                            ins.then_inc(s_xnu, 1)

            def gates(name, l, w):
                pe.wait_ge(s_mr, 1)
                for b in range(B):
                    dst = begin((name, b))
                    q = 64 * l + 32 * w
                    nc.tensor.matmul(dst, sel[q:q + B, b], MR[q:q + B], start=True, stop=True).then_inc(s_mm, 1)

            pe.wait_ge(s_ident, 16)
            for j in FIRST:
                mod_row(0, j)
            for j in FIRST:
                mod_column(0, j)
            norm(0)
            pe.wait_ge(s_wqkvl, 1)
            for i, key in enumerate(PROJECTIONS):
                b = key[1]
                cols = slice(b * S, (b + 1) * S)
                dst = begin(key)
                if key[0] == "v":
                    pe.wait_ge(s_free, J["vt", b] + 1)
                    for ti in range(TB):
                        ins = nc.tensor.transpose(dst[:, ti * P:(ti + 1) * P], VT[:, ti * P:(ti + 1) * P], ident[:])
                else:
                    if key[0] == "q" and key[2] == 0:
                        pe.wait_ge(s_free, J["norm", 0, b, KC - 1] + 1)
                    at_col = {"q": key[-1] * P, "k": D, "vt": D + KVW}[key[0]]
                    ins = product(dst, pair(WQKVH, WQKVL, slice(at_col, at_col + P)), h_cols(cols))
                ins.then_inc(s_mm, 1)
                for row in row_after(i):
                    mod_row(*row)
                for row in column_after(i):
                    mod_column(*row)
            pe.wait_ge(s_const, 16 * 4)
            dst = begin(("gsum",))
            pe.wait_ge(s_free, J["modrow", 1, 5] + 1)
            for g in range(4):
                ins = nc.tensor.matmul(dst[32 * g:32 * g + 32], sumsel[:], MRG[:, g], start=True, stop=True,
                                       tile_position=(0, 32 * g))
            ins.then_inc(s_mm, 1)

            units = B * GROUPS * TB
            pe.wait_ge(s_free, J["ga0", 0])
            pe.wait_ge(s_silu, 3)
            blocks = [0, 0]

            def scores(n):
                q, ic = divmod(n, TB)
                if ic == 0:
                    pe.wait_ge(s_qks[q % STACKS], 128 * (q // STACKS + 1))
                for half in range(2):
                    if n >= 1:
                        pe.wait_ge(s_mx, 2 * (n - 1) + half + 1)
                    for h in (2 * half, 2 * half + 1):
                        nc.tensor.matmul(PS[:, h, 0:(ic + 1) * P], QS[:, q % STACKS, h, ic * P:(ic + 1) * P],
                                         KS[:, q % STACKS, 0:(ic + 1) * P], start=True, stop=True)
                        ins = nc.tensor.matmul(PS[:, h, ic * P:(ic + 1) * P], identB[:], maskB[:], start=False, stop=True,
                                               skip_group_check=True)
                    ins.then_inc(s_s, 1)

            def transposed(n):
                q, ic = divmod(n, TB)
                for jc in range(ic + 1):
                    i = blocks[0]
                    if i >= 3:
                        pe.wait_ge(s_exp, i - 2)
                    dst = PS[:, 4 + i % 3]
                    nc.tensor.matmul(dst, KS[:, q % STACKS, jc * P:(jc + 1) * P], QS[:, q % STACKS, :, ic * P:(ic + 1) * P],
                                     start=True, stop=False)
                    if jc == ic:
                        nc.tensor.matmul(dst, maskB[:], identB[:].unsqueeze(1).to_broadcast([P, REP, P]),
                                         start=False, stop=False)
                    if jc == 0:
                        pe.wait_ge(s_dg, n + 1)
                    nc.tensor.matmul(dst, onesR[:], DG[:, n % 2], start=False, stop=True).then_inc(s_st, 1)
                    blocks[0] += 1

            def weighted(n):
                q, ic = divmod(n, TB)
                b, g = divmod(q, GROUPS)
                if ic == 0 and q:
                    pe.wait_ge(s_ot, q)
                for jc in range(ic + 1):
                    blocks[1] += 1
                    pe.wait_ge(s_exp, blocks[1])
                    for h in range(REP):
                        ins = nc.tensor.matmul(PS[32 * h:32 * h + 32, 7, ic * P:(ic + 1) * P],
                                               V[:, b * TB + jc, g].rearrange("p a d -> p (a d)"), PT[:, n % 2, jc, h],
                                               start=(jc == 0), stop=(jc == ic), tile_position=(0, 32 * h))
                ins.then_inc(s_pv, 1)

            for n in range(units + 3):
                if n < units:
                    scores(n)
                if 2 <= n < units + 2:
                    transposed(n - 2)
                if n >= 3:
                    weighted(n - 3)
            pe.wait_ge(s_mx, 2 * units)
            pe.wait_ge(s_ot, B * GROUPS)
            pe.wait_ge(s_exp, blocks[0])

            gates("ga0", 0, 0)
            pe.wait_ge(s_w0l, 1)
            for t in range(NT):
                if t % TB == 0:
                    pe.wait_ge(s_oL1 if t else s_oL, REP)
                product(begin(("wo", t)), f_cols(slice(t * P, (t + 1) * P)), pair(WOH, WOL, slice(0, D))
                        ).then_inc(s_mm, 1)
            norm(1)
            pe.wait_ge(s_w0p, 1)
            for b in range(B):
                pe.wait_ge(s_free, J["norm", 1, b, KC - 1] + 1)
                product(begin(("rq", b)), pair(RQH, RQL, slice(0, P)), h_cols(slice(b * S, (b + 1) * S))
                        ).then_inc(s_mm, 1)
            for b in range(B):
                dst = begin(("score", b))
                pe.wait_ge(s_free, J["rq", b] + 1)
                for ti in range(TB):
                    t = b * TB + ti
                    ins = nc.tensor.matmul(dst[:, ti * EXPERTS:(ti + 1) * EXPERTS], RQ[:, t * P:(t + 1) * P], KEYS[:],
                                           start=True, stop=True)
                ins.then_inc(s_mm, 1)
            gates("gb0", 0, 1)
            pe.wait_ge(s_w0p, 2)
            for i in range(NT + LAG + 1):
                if i == LAG + 1:
                    pe.wait_ge(s_w0p, 3)
                if i < NT:
                    product(begin(("z", i)), h_cols(slice(i * P, (i + 1) * P)), pair(ATH, ATL, slice(0, D))
                            ).then_inc(s_mm, 1)
                if 0 <= i - LAG < NT:
                    t = i - LAG
                    dst = begin(("zt", t))
                    pe.wait_ge(s_free, J["z", t] + 1)
                    for c in range(KC):
                        ins = nc.tensor.transpose(dst[:, c * P:(c + 1) * P], XN[1][:, t % 4, c * P:(c + 1) * P],
                                                  ident[:])
                    ins.then_inc(s_mm, 1)
                if i > LAG:
                    t = i - LAG - 1
                    dst = begin(("y", t))
                    pe.wait_ge(s_free, J["zt", t] + 1)
                    product(dst, f_cols(slice(t * P, (t + 1) * P)), pair(BTH, BTL, slice(0, D))
                            ).then_inc(s_mm, 1)
            norm(2)

            def inner(key, weights):
                cols = slice(key[1] * S, (key[1] + 1) * S)
                product(begin(key), lambda k: tuple(weights[:, i, k * P:(k + 1) * P] for i in range(2)),
                        (f_cols if key[0] == "to" else h_cols)(cols)).then_inc(s_mm, 1)

            def outer(dst, weights, b):
                nc.tensor.matmul(dst, weights[0], TL[:, b * S:(b + 1) * S], start=False, stop=False)
                return nc.tensor.matmul(dst, weights[1], TL[:, b * S:(b + 1) * S], start=False, stop=True)

            for b in range(B):
                pe.wait_ge(s_free, J["norm", 2, b, KC - 1] + 1)
                if b == 0:
                    pe.wait_ge(s_pl, 1)
                    pe.wait_ge(s_ll, 1)
                inner(("tqkv", b), LQ)
                for m in range(KC):
                    dst = begin(("qkv", b, m))
                    product(dst, pair(WQH, WQL, slice(m * P, (m + 1) * P)), h_cols(slice(b * S, (b + 1) * S)), stop=False)
                    pe.wait_ge(s_free, J["tqkv", b] + 1)
                    outer(dst, [LQ[:, i, KC * P + m * P:KC * P + (m + 1) * P] for i in range(2)], b).then_inc(s_mm, 1)
            pe.wait_ge(s_pl, 2)
            pe.wait_ge(s_ll, 2)
            for b in range(B):
                pe.wait_ge(s_free, J["qkv", b, KC - 1] + 1)
                inner(("to", b), LOA)
                for m in range(KC):
                    dst = begin(("o", b, m))
                    product(dst, pair(W2H, W2L, slice(m * P, (m + 1) * P)), f_cols(slice(b * S, (b + 1) * S)), stop=False)
                    pe.wait_ge(s_free, J["to", b] + 1)
                    outer(dst, [LOB[:, i, m * P:(m + 1) * P] for i in range(2)], b).then_inc(s_mm, 1)
            for b in range(B):
                pe.wait_ge(s_free, J["o", b, KC - 1] + 1)
                pe.wait_ge(s_ll, 3)
                inner(("tgu", b), LGA)
            for n in range(2):
                for m in range(MC):
                    p = GU_START[n] + m
                    pe.wait_ge(s_wl, ring_no(p))
                    for b in range(B):
                        if n and m == 0:
                            pe.wait_ge(s_free, J["norm", 3, b, KC - 1] + 1)
                        for mat in range(2):
                            dst = begin(("gu", n, m, b, mat))

                            def w(k):
                                off = (mat * KC + k) * P
                                return WRH[:, slot(p), off:off + P], WRL[:, slot(p), off:off + P]

                            ins = product(dst, w, h_cols(slice(b * S, (b + 1) * S)), stop=bool(n))
                            if n == 0:
                                pe.wait_ge(s_free, J["tgu", B - 1] + 1)
                                off = PW + mat * P
                                ins = outer(dst, [r[:, slot(p), off:off + P] for r in (WRH, WRL)], b)
                            ins.then_inc(s_mm, 1)
                if n == 0:
                    pe.wait_ge(s_ldw, 16)
                    for b in range(B):
                        dst = begin(("td", b))
                        for k in range(MC):
                            pe.wait_ge(s_free, J["gu", n, k, b, 1] + 1)
                            q = 32 * (k % 4)
                            ins = nc.tensor.matmul(dst[q:q + 32], LDA[:, k], HID[:, k, b * S:(b + 1) * S],
                                                   start=(k < 4), stop=(k >= MC - 4), tile_position=(0, q))
                        ins.then_inc(s_mm, 1)
                gates(f"g{n}", 1, n)
                dst = [begin(("down", n, t)) for t in range(NT)]
                if n == 0:
                    for c in range(KC):
                        for t in range(NT):
                            for part in (HH, HL):
                                ins = nc.tensor.matmul(dst[t][:, c * P:(c + 1) * P], part[:, c, t * P:(t + 1) * P],
                                                       identR[:], start=(part is HH and c == 0), stop=False,
                                                       skip_group_check=True)
                        ins.then_inc(s_x1u, 1)
                for k in range(MC):
                    p = DN_START[n] + k // 2
                    pe.wait_ge(s_wl, ring_no(p))
                    hidden_is_split(pe, n, k)
                    w = slice(k % 2 * D, (k % 2 + 1) * D)
                    for t in range(NT):
                        cols = slice(t * P, (t + 1) * P)
                        hh, hl = HH[:, k % 4, cols], HL[:, k % 4, cols]
                        wh, wl = WRH[:, slot(p), w], WRL[:, slot(p), w]
                        last = k == MC - 1
                        nc.tensor.matmul(dst[t], hh, wh, start=(n == 1 and k == 0), stop=False, skip_group_check=True)
                        nc.tensor.matmul(dst[t], hh, wl, start=False, stop=False, skip_group_check=True)
                        ins = nc.tensor.matmul(dst[t], hl, wh, start=False, stop=last and n == 1, skip_group_check=True)
                        if last and n == 0:
                            if t == 0:
                                pe.wait_ge(s_ldl, 1)
                                pe.wait_ge(s_free, J["td", B - 1] + 1)
                            nc.tensor.matmul(dst[t], TDH[:, cols], LDBH[:], start=False, stop=False,
                                             skip_group_check=True)
                            nc.tensor.matmul(dst[t], TDL[:, cols], LDBH[:], start=False, stop=False,
                                             skip_group_check=True)
                            ins = nc.tensor.matmul(dst[t], TDH[:, cols], LDBL[:], start=False, stop=True,
                                                   skip_group_check=True)
                        if last:
                            ins.then_inc(s_mm, 1)
                    if not last:
                        ins.then_inc(s_hsu, 1)
                if n == 0:
                    norm(3)


def layout(x):
    def f(name):
        return np.asarray(x[name])

    def pad_cols(m, copies, width):
        out = np.zeros((m.shape[0], P), m.dtype)
        for off in copies:
            out[:, off:off + m.shape[1]] = m
        return out.reshape(-1, P, P).transpose(1, 0, 2)

    def pad_rows(m, copies):
        out = np.zeros((P, m.shape[1]), m.dtype)
        for off in copies:
            out[off:off + m.shape[0]] = m
        return out

    halves, quadrants = (0, 64), (0, 32, 64, 96)
    r = {"X": f("L0_attn_x").reshape(T, D)}
    r["WQ"] = f("L0_attn_wq").reshape(D, GROUPS, REP, HD).transpose(0, 2, 1, 3).reshape(D, D)
    r["WK"], r["WV"] = f("L0_attn_wk"), f("L0_attn_wv")
    r["WO"] = f("L0_attn_wo").reshape(GROUPS, REP, HD, D).transpose(1, 0, 2, 3).reshape(D, D)
    r["AT"], r["BT"] = f("L0_ffn_A_w").T, f("L0_ffn_B_w").T
    r["RQ"] = pad_cols(f("L0_ffn_Wq_w").T, (0,), P)
    r["KEYS"] = f("L0_ffn_keys").T
    r["CT"] = np.stack([f(f"L{l}_c").T.reshape(KC, P, B).transpose(1, 0, 2) for l in range(2)], 1)
    r["WM0"], r["WM1"] = f("L0_wmod"), f("L1_wmod")

    def attn(codes):
        return codes.reshape(D, 2, 2, P).transpose(1, 3, 2, 0).reshape(2, P, PW)

    def attn_s(s):
        return s.reshape(D, 2, 2, 2).transpose(1, 3, 2, 0).reshape(2, 2, PW)

    def gu(g, u):
        return np.stack([g, u]).reshape(2, MC, P, KC, P).transpose(1, 4, 0, 3, 2).reshape(MC, P, PW)

    def gu_s(g, u):
        return np.stack([g, u]).reshape(2, MC, P, KC, 2).transpose(1, 4, 0, 3, 2).reshape(MC, 2, PW)

    def down(w):
        return w.reshape(D, MC // 2, 2, P).transpose(1, 3, 2, 0).reshape(MC // 2, P, PW)

    def down_s(s):
        return s.reshape(D, MC // 2, 2, 2).transpose(1, 3, 2, 0).reshape(MC // 2, 2, PW)

    ca, sa = f("L1_attn_codes_attn"), f("L1_attn_scales_attn")
    ac, asc = [attn(ca[i]) for i in range(4)], [attn_s(sa[i]) for i in range(4)]
    cg, sg = f("L1_attn_codes_gu"), f("L1_attn_scales_gu")
    per = D // 64
    r["CODES"] = np.concatenate(
        [np.stack([ac[m][h] for m in range(3) for h in range(2)]), ac[3], gu(cg[0], cg[1]),
         down(f("L1_attn_codes_down")), gu(f("L1_ffn_gate_q"), f("L1_ffn_up_q")), down(f("L1_ffn_down_q"))])
    r["SCALES"] = np.concatenate(
        [np.stack([asc[m][h] for m in range(3) for h in range(2)]), asc[3], gu_s(sg[0], sg[1]),
         down_s(f("L1_attn_scales_down")),
         gu_s(f("L1_ffn_gate_absmax").reshape(MLP, per), f("L1_ffn_up_absmax").reshape(MLP, per)),
         down_s(f("L1_ffn_down_absmax").reshape(D, MLP // 64))])
    A, Bm = f("L1_attn_lora_A_h"), f("L1_attn_lora_B_attn")
    cat = np.concatenate
    r["LQKV"] = cat([pad_cols(cat(list(A[0:3])).T, halves, P).reshape(P, KC * P),
                     pad_rows(cat([Bm[i].T for i in range(3)]), halves)], 1)
    r["LO"] = cat([pad_cols(A[3].T, halves, P).reshape(P, KC * P), pad_rows(Bm[3].T, halves)], 1)
    r["LGA"] = pad_cols(cat([A[4], A[5]]).T, halves, P).reshape(P, KC * P)
    bg = f("L1_attn_lora_B_gu")
    lb = np.zeros((P, 2, MLP), bg.dtype)
    for off in halves:
        for mat in range(2):
            lb[off + LR * mat:off + LR * (mat + 1), mat] = bg[mat].T
    r["LBGU"] = lb.reshape(P, 2, MC, P).transpose(2, 0, 1, 3).reshape(MC, P, LBW)
    ad = f("L1_attn_lora_A_down")
    lda = np.zeros((P, MC, 2 * LR), ad.dtype)
    lda[:, :, 0:LR] = ad.T.reshape(MC, P, LR).transpose(1, 0, 2)
    r["LDA"] = lda
    r["LDB"] = pad_rows(f("L1_attn_lora_B_down").T, quadrants)
    eye = np.eye(P, dtype=np.float32)
    r["IDENT"] = eye
    sel, sumsel = np.zeros((P, B, P), np.float32), np.zeros((P, 32), np.float32)
    for q in range(0, P, 32):
        for b in range(B):
            sel[q + b, b] = 1.0
            sumsel[q + b, b] = 1.0
    r["SEL"], r["SUMSEL"] = sel, sumsel
    bf16 = mybir.dt.np(BF16)
    r["IDENTB"] = eye.astype(bf16)
    r["MASKB"] = np.where(np.arange(P)[None, :] > np.arange(P)[:, None], MASKED, 0.0).astype(bf16)
    return {k: np.ascontiguousarray(v) for k, v in r.items()}


def kernel(**inputs):
    import concourse.bacc as bacc
    from concourse.bass_utils import run_bass_kernel_spmd

    nc = bacc.Bacc("TRN2", target_bir_lowering=False, num_devices=1)
    arrays = layout(inputs)
    a = {k: nc.dram_tensor(f"in_{k}", v.shape, mybir.dt.from_np(v.dtype), kind="ExternalInput").ap()
         for k, v in arrays.items()}
    out = nc.dram_tensor("out_x", (T, D), F32, kind="ExternalOutput").ap()
    build(nc, a, out)
    r = run_bass_kernel_spmd(nc, [{f"in_{k}": v for k, v in arrays.items()}], core_ids=[0])
    return r.results[0]["out_x"].reshape(B, S, D)
```
